# Optimizing a Trainium2 kernel written in Bass

```python
import numpy as np
import jax
import jax.numpy as jnp

def _softmax(x, axis=-1):
    return jax.nn.softmax(x, axis=axis)

def _gelu(x):
    return jax.nn.gelu(x, approximate=True)

def _silu(x):
    return jax.nn.silu(x)

def _sigmoid(x):
    return jax.nn.sigmoid(x)

def _layernorm(x, axis=-1, eps=1e-05):
    m = jnp.mean(x, axis=axis, keepdims=True)
    v = jnp.var(x, axis=axis, keepdims=True)
    return (x - m) / jnp.sqrt(v + eps)

def _scatter_add(tgt, idx, src, axis=0):
    return tgt.at[idx].add(src)

def _segment_sum(src, seg, n):
    return jax.ops.segment_sum(src, seg, n)
kernel_name = 'mk_lm_tower_d1_tok_ids1024_r4_9ceb83'

def setup_inputs(seed: int=0):
    np.random.seed(seed)
    _w = jnp.asarray

    def _rec_inputs():
        import jax
        import jax.numpy as jnp
        _rk = jax.random.key(seed)
        x = jax.random.randint(jax.random.fold_in(_rk, 1), (8, 512), 0, 12564, jnp.int32)
        return x
    x = _rec_inputs()

    def _L0_tok_setup():
        import jax, jax.numpy as jnp
        import numpy as np
        SCALING = 16.0 / 8.0
        key = jax.random.key(seed)
        k1, k2, k3, k4 = jax.random.split(key, 4)
        V, D, R = (50257, 256, 8)
        B, S = (8, 512)
        x = jax.random.randint(k1, (B, S), 0, V, dtype=jnp.int32)
        W = jax.random.normal(k2, (V, D), dtype=jnp.float32)
        lora_A = jax.random.normal(k3, (R, V), dtype=jnp.float32)
        lora_B = jax.random.normal(k4, (D, R), dtype=jnp.float32)
        return {'x': x, 'W': W, 'lora_A': lora_A, 'lora_B': lora_B}
    _L0_tok_all = _L0_tok_setup()
    _L0_tok_in = {k: v for k, v in _L0_tok_all.items() if k in ('W', 'lora_A', 'lora_B')}
    del _L0_tok_all

    def _L0_attn_setup():
        import jax, jax.numpy as jnp
        import numpy as np
        PI = float(np.pi)
        EPS = 1e-06
        key = jax.random.key(seed)
        k1, k2, k3, k4, k5 = jax.random.split(key, 5)
        B, T, D, H, Dh = (4, 1024, 256, 16, 64)

        def xavier(k, shape):
            fan_in, fan_out = (shape[-2], shape[-1])
            lim = float(np.sqrt(6.0 / (fan_in + fan_out)))
            return jax.random.uniform(k, shape, jnp.float32, -lim, lim)
        return {'query': jax.random.normal(k1, (B, T, D), jnp.float32), 'W_Q': xavier(k2, (H, D, 1)), 'W_K': xavier(k3, (H, D, 1)), 'W_V': xavier(k4, (H, D, Dh)), 'W_O': xavier(k5, (D, Dh, H))}
    _L0_attn_all = _L0_attn_setup()
    _L0_attn_in = {k: v for k, v in _L0_attn_all.items() if k in ('W_Q', 'W_K', 'W_V', 'W_O')}
    del _L0_attn_all

    def _L0_ffn_setup():
        import jax, jax.numpy as jnp
        import numpy as np
        ALPHA = 1.0
        key = jax.random.key(seed)
        ks = jax.random.split(key, 7)
        B, S, IN, OUT = (8, 2048, 256, 256)
        RANK, DDIM, UDIM = (4, 100, 50)
        return {'hidden_states': jax.random.normal(ks[0], (B, S, IN), dtype=jnp.float32), 'W': jax.random.normal(ks[1], (OUT, IN), dtype=jnp.float32) * 0.02, 'b': jax.random.normal(ks[2], (OUT,), dtype=jnp.float32) * 0.02, 'lora_down': jax.random.normal(ks[3], (RANK, DDIM), dtype=jnp.float32) * 0.1, 'lora_up': jax.random.normal(ks[4], (UDIM, RANK), dtype=jnp.float32) * 0.1, 'down_aux': jax.random.normal(ks[5], (DDIM, IN), dtype=jnp.float32) * 0.03, 'up_aux': jax.random.normal(ks[6], (OUT, UDIM), dtype=jnp.float32) * 0.03}
    _L0_ffn_all = _L0_ffn_setup()
    _L0_ffn_in = {k: v for k, v in _L0_ffn_all.items() if k in ('W', 'b', 'lora_down', 'lora_up', 'down_aux', 'up_aux')}
    del _L0_ffn_all
    return {'x': x, 'L0_tok_W': _L0_tok_in['W'], 'L0_tok_lora_A': _L0_tok_in['lora_A'], 'L0_tok_lora_B': _L0_tok_in['lora_B'], 'L0_attn_W_Q': _L0_attn_in['W_Q'], 'L0_attn_W_K': _L0_attn_in['W_K'], 'L0_attn_W_V': _L0_attn_in['W_V'], 'L0_attn_W_O': _L0_attn_in['W_O'], 'L0_ffn_W': _L0_ffn_in['W'], 'L0_ffn_b': _L0_ffn_in['b'], 'L0_ffn_lora_down': _L0_ffn_in['lora_down'], 'L0_ffn_lora_up': _L0_ffn_in['lora_up'], 'L0_ffn_down_aux': _L0_ffn_in['down_aux'], 'L0_ffn_up_aux': _L0_ffn_in['up_aux']}

def reference(x, L0_tok_W, L0_tok_lora_A, L0_tok_lora_B, L0_attn_W_Q, L0_attn_W_K, L0_attn_W_V, L0_attn_W_O, L0_ffn_W, L0_ffn_b, L0_ffn_lora_down, L0_ffn_lora_up, L0_ffn_down_aux, L0_ffn_up_aux):
    import jax
    import jax.numpy as jnp

    def _L0_tok_ref(x, W, lora_A, lora_B):
        import jax, jax.numpy as jnp
        import numpy as np
        SCALING = 16.0 / 8.0
        base = W[x]
        A_g = lora_A[:, x]
        delta = jnp.einsum('dr,rbs->bsd', lora_B, A_g) * SCALING
        return base + delta

    def _L0_attn_ref(query, W_Q, W_K, W_V, W_O):
        import jax, jax.numpy as jnp
        import numpy as np
        PI = float(np.pi)
        EPS = 1e-06
        q = jnp.einsum('btd,hdo->btho', query, W_Q)
        k = jnp.einsum('btd,hdo->btho', query, W_K)
        V = jnp.einsum('btd,hde->bthe', query, W_V)
        q = jnp.tanh(q) * (PI / 4)
        k = jnp.tanh(k) * (PI / 4)
        cos_k, sin_k = (jnp.cos(k), jnp.sin(k))
        cos_q, sin_q = (jnp.cos(q), jnp.sin(q))
        cos_KV = jnp.cumsum(cos_k * V, axis=1)
        sin_KV = jnp.cumsum(sin_k * V, axis=1)
        heads = cos_q * cos_KV + sin_q * sin_KV
        cos_K = jnp.cumsum(cos_k, axis=1)
        sin_K = jnp.cumsum(sin_k, axis=1)
        denom = cos_q * cos_K + sin_q * sin_K + EPS
        heads = heads / denom
        return jnp.einsum('deh,bthe->btd', W_O, heads)

    def _L0_ffn_ref(hidden_states, W, b, lora_down, lora_up, down_aux, up_aux):
        import jax, jax.numpy as jnp
        import numpy as np
        ALPHA = 1.0
        lilora_weight = up_aux @ (lora_up @ (lora_down @ down_aux))
        base = jnp.einsum('bsi,oi->bso', hidden_states, W) + b
        delta = jnp.einsum('bsi,oi->bso', hidden_states, lilora_weight)
        return base + ALPHA * delta
    h = _L0_tok_ref(x, L0_tok_W, L0_tok_lora_A, L0_tok_lora_B)
    h = h + _L0_attn_ref(_layernorm(h, axis=-1), L0_attn_W_Q, L0_attn_W_K, L0_attn_W_V, L0_attn_W_O)
    h = h + _L0_ffn_ref(_layernorm(h, axis=-1), L0_ffn_W, L0_ffn_b, L0_ffn_lora_down, L0_ffn_lora_up, L0_ffn_down_aux, L0_ffn_up_aux)
    return h

_drawn_inputs = setup_inputs


def setup_inputs(seed=0):
    import zlib

    import numpy as np

    out = dict(_drawn_inputs(seed))
    spreads = {}
    factors = {'L0_ffn_b': 178.407,
     'L0_ffn_lora_down': 8.0,
     'L0_ffn_lora_up': 8.0,
     'L0_ffn_down_aux': 8.0,
     'L0_ffn_up_aux': 8.0,
     'L0_ffn_W': 8.0}
    for name, (base, spread) in spreads.items():
        noise = np.random.default_rng([zlib.crc32(name.encode()), seed]).standard_normal(out[name].shape)
        drawn = base * np.exp(spread * noise) if base else spread * noise
        out[name] = jnp.asarray(drawn.astype(out[name].dtype))
    for name, factor in factors.items():
        out[name] = (out[name] * factor).astype(out[name].dtype)
    return out
```

```python
from contextlib import ExitStack

import concourse.bass as bass
from concourse import mybir

F32 = mybir.dt.float32
F32R = mybir.dt.float32r
I32 = mybir.dt.int32
ALU = mybir.AluOpType
ACT = mybir.ActivationFunctionType

P = 128
BATCHES = 8
C = 4
T = C * P
D = 256
KD = D // P
H = 16
E = 64
HE = H * E
PAIRS = HE // P
G = 4
HG = H // G
FEAT = 2
R = 8
COPIES = 4
QKV = HE + 2 * H
THIRD = QKV // 3
VLAST = HE - 2 * THIRD
ROW = D + R
LN_EPS = 1e-5
DEN_EPS = 1e-6
LORA_SCALE = 16.0 / 8.0
QUARTER_PI = 3.141592653589793 / 4

SMALL_LOADS = 4 + COPIES + 2

C_CAUSAL, C_ONES, C_IDENT = 0, P, 2 * P
C_LO_K, C_LO_Q, C_HEAD, C_HALFPI = 3 * P, 3 * P + 1, 3 * P + 2, 3 * P + 2 + HG
C_EPS, C_POWER = C_HALFPI + 1, C_HALFPI + 2
N_CONST = C_POWER + 1


class Batch:

    def __init__(self, fixed, reg=None):
        self.fixed, self.reg = fixed, reg
        self.parity = fixed % 2

    def __add__(self, n):
        return Batch(self.fixed + n, self.reg)

    def times(self, n, k=0):
        v = self.fixed * n + k
        return v if self.reg is None else self.reg * (2 * n) + v


def done(b, per, k):
    return b.times(per, k)


def done_parity(b, per, k):
    v = (b.fixed // 2) * per + k
    return v if b.reg is None else b.reg * per + v


def tower(nc, idx, table, wqkv, wo, wff, ld_t, lu_t, da, ua_t, lb_t, bias, consts, out):
    with ExitStack() as ctx:
        def sb(name, shape, dt=F32):
            return ctx.enter_context(nc.sbuf_tensor(name, shape, dt))

        def sem(name):
            return ctx.enter_context(nc.semaphore(name))

        cst = sb("cst", [P, N_CONST])
        causal, ones, ident = (cst[:, o:o + P] for o in (C_CAUSAL, C_ONES, C_IDENT))
        lo_k, lo_q = cst[:, C_LO_K:C_LO_K + 1], cst[:, C_LO_Q:C_LO_Q + 1]
        idx_sb = sb("idx_sb", [P, BATCHES * C], I32)
        idx_cur = sb("idx_cur", [P, 2, C], I32)
        idx_seen = sb("idx_seen", [P, C], I32)
        wqkv_hi, wqkv_lo = (sb(f"wqkv_{n}", [P, KD, QKV], F32R) for n in ("hi", "lo"))
        wo_hi, wo_lo = (sb(f"wo_{n}", [P, PAIRS, D], F32R) for n in ("hi", "lo"))
        wff_hi, wff_lo = (sb(f"wff_{n}", [P, KD, D], F32R) for n in ("hi", "lo"))
        lb_stack = sb("lb_stack", [P, D], F32R)
        bias_sb = sb("bias_sb", [P, D])
        emb = sb("emb", [P, 2, C, ROW])
        a_rep = sb("a_rep", [P, C, P])
        a_stack = sb("a_stack", [P, T], F32R)
        h1 = sb("h1", [P, 2, C, D])
        h2 = sb("h2", [P, C, D])
        y1, y2 = sb("y1", [P, C, D]), sb("y2", [P, C, D])
        y1_hi, y1_lo = (sb(f"y1_{n}", [P, KD, T], F32R) for n in ("hi", "lo"))
        y2_hi, y2_lo = (sb(f"y2_{n}", [P, KD, T], F32R) for n in ("hi", "lo"))
        ln = [sb(f"ln{i}", [P, C, 6]) for i in (1, 2)]
        ln_mv = [sb(f"ln_mv{i}", [P, C, 2]) for i in (1, 2)]
        ln_ve = [sb(f"ln_ve{i}", [P, C]) for i in (1, 2)]
        ln_rstd = [sb(f"ln_rstd{i}", [P, C]) for i in (1, 2)]
        V = sb("V", [P, C, HE])
        th = sb("th", [P, C, 2 * H])
        fq, fk = sb("fq", [P, C, H * FEAT]), sb("fk", [P, C, H * FEAT])
        prod = sb("prod", [P, C, H * FEAT])
        den, rden = sb("den", [P, C * H]), sb("rden", [P, C * H])
        fqn = sb("fqn", [P, C, H * FEAT])
        k_rep, q_rep = sb("k_rep", [P, C, P]), sb("q_rep", [P, C, P])
        round_hi = sb("round_hi", [P, T], F32R)
        k_mix, q_mix = sb("k_mix", [P, T]), sb("q_mix", [P, T])
        k_group = sb("k_group", [P, G, T], F32R)
        q_group = sb("q_group", [P, G, T], F32R)
        q_head = sb("q_head", [P, HG, T], F32R)
        wts = sb("wts", [P, 2, H, P])
        st_mask = sb("st_mask", [P, HG, E])
        st_hi = sb("st_hi", [P, HG * E], F32R)
        st = sb("st", [P, HG * E], F32R)
        at_hi, at_lo = (sb(f"at_{n}", [P, PAIRS, C, P], F32R) for n in ("hi", "lo"))
        outb = sb("outb", [P, 2, C, D])
        raw_qkv = V[:, :, :].rearrange("p c n -> p (c n)")[:, 0:KD * QKV].rearrange("p (k n) -> p k n", k=KD)
        raw = wts[:, :, :, :].rearrange("p a h t -> p (a h t)")
        raw_wo = raw[:, 0:PAIRS * D].rearrange("p (k n) -> p k n", k=PAIRS)
        raw_ff = raw[:, PAIRS * D:(PAIRS + KD) * D].rearrange("p (k n) -> p k n", k=KD)
        small = h2[:, :, :]
        raw_da, raw_ua, raw_lb, low2 = (small[:, i, :] for i in range(4))
        small_b = y2[:, :, :]
        raw_ld, raw_lu, low1, lb2 = (small_b[:, i, :] for i in range(4))

        ps = ctx.enter_context(nc.psum_tensor("ps", [P, 8, 512], F32))
        heads_ps = [ps[:, 0:2, :].rearrange("p a (b t) -> p (a b) t", t=P),
                    ps[:, 3:5, :].rearrange("p a (b t) -> p (a b) t", t=P)]
        proj_ps = [ps[:, 3 + i, :].rearrange("p (c n) -> p c n", n=D) for i in range(2)]
        state_ps = ps[:, 2, 0:HG * E]
        misc = ps[:, 7, :]
        misc_pair = misc.rearrange("p (c n) -> p c n", n=D)

        s_cst, s_idx, s_wqkv, s_wo, s_small = (sem(n) for n in ("cst_loaded", "idx_loaded", "wqkv_loaded", "wo_loaded", "small_loaded"))
        s_zero, s_low, s_whi, s_wdone, s_lb2, s_lbhi = (
            sem(n) for n in ("zeros_ready", "low_rank_mm", "w_hi_ready", "w_ready", "lb2_ready", "lb_hi_ready"))
        s_lowc, s_wff, s_lbs = sem("low_rank_copied"), sem("wff_whole"), sem("lb_stack_ready")
        s_idxc = sem("idx_copied")
        s_gather = [sem(f"gathered{i}") for i in range(2)]
        s_arep, s_atp, s_ahi, s_ast, s_lora, s_h1 = (
            sem(n) for n in ("a_rep_ready", "a_turned", "a_hi_ready", "a_stack_ready", "lora_mm", "h1_ready"))
        s_stats = [sem(f"ln{i}_stats") for i in (1, 2)]
        s_mv = [sem(f"ln{i}_mean_var") for i in (1, 2)]
        s_ve = [sem(f"ln{i}_var_eps") for i in (1, 2)]
        s_rstd = [sem(f"ln{i}_rstd") for i in (1, 2)]
        s_y = [sem(f"y{i}_ready") for i in (1, 2)]
        s_ytp = [sem(f"y{i}_turned") for i in (1, 2)]
        s_yhi = [sem(f"y{i}_hi_ready") for i in (1, 2)]
        s_ylo = [sem(f"y{i}_lo_ready") for i in (1, 2)]
        s_vmm, s_vev, s_fk, s_fq, s_cumk = (
            sem(n) for n in ("qkv_mm", "qkv_copied", "k_features", "q_features", "k_sums_mm"))
        s_krep, s_prod, s_den, s_rden, s_fqn, s_qrep = (
            sem(n) for n in ("k_rep_ready", "den_products", "den_ready", "rden_ready", "fqn_ready", "q_rep_ready"))
        s_ktp, s_khi, s_kmix, s_kgrp = (sem(n) for n in ("k_turned", "k_hi_ready", "k_mix_ready", "k_group_ready"))
        s_qtp, s_qhi, s_qmix, s_qhead, s_qgrp = (
            sem(n) for n in ("q_turned", "q_hi_ready", "q_mix_ready", "q_head_ready", "q_group_ready"))
        s_wmm, s_wts, s_at = sem("weights_mm"), sem("weights_masked"), sem("attention_mm")
        s_stmm, s_stm, s_sthi, s_st = (
            sem(n) for n in ("state_mm", "state_masked", "state_hi_ready", "state_ready"))
        s_athi, s_atlo = sem("at_hi_ready"), sem("at_lo_ready")
        s_omm, s_h2, s_h2b, s_ffmm, s_out = (
            sem(n) for n in ("proj_mm", "h2_ready", "h2_bias_added", "ffn_mm", "out_ready"))
        s_stored = [sem(f"stored{i}") for i in range(2)]

        def iterations(eng, run):
            run(Batch(0), True, False)
            with eng.Fori(0, (BATCHES - 2) // 2) as i:
                run(Batch(1, i), False, False)
                run(Batch(2, i), False, False)
            run(Batch(BATCHES - 1), False, True)

        block = ctx.enter_context(nc.Block())

        @block.sync
        def _(sp):
            for i in range(2):
                sp.sem_inc(s_stored[i], 16)
            sp.dma_start(idx_sb[:, :], idx).then_inc(s_idx, 16)
            sp.dma_start(cst[:, :], consts).then_inc(s_cst, 16)
            sp.dma_start(raw_qkv, wqkv.rearrange("(k p) n -> p k n", p=P)).then_inc(s_wqkv, 16)
            sp.dma_start(raw_wo, wo.rearrange("(k p) n -> p k n", p=P)).then_inc(s_wo, 16)
            sp.wait_ge(s_zero, 1)
            for dst, src in ((raw_da, da), (raw_ua, ua_t), (raw_ld, ld_t), (raw_lu, lu_t)):
                sp.dma_start(dst[0:src.shape[0], 0:src.shape[1]], src).then_inc(s_small, 16)
            for c in range(COPIES):
                sp.dma_start(raw_lb[R * c:R * (c + 1), :], lb_t).then_inc(s_small, 16)
            sp.dma_start(raw_ff, wff.rearrange("(k p) n -> p k n", p=P)).then_inc(s_small, 16)
            sp.dma_start(bias_sb[:, :], bias.partition_broadcast(P)).then_inc(s_small, 16)

            def store(b):
                sp.wait_ge(s_out, done(b, 2, 2))
                rows = out[bass.ds(b.times(T), T), :].rearrange("(c p) n -> p c n", p=P)
                sp.dma_start(rows, outb[:, b.parity, :, :]).then_inc(s_stored[b.parity], 16)

            def run(b, first, last):
                if not first:
                    store(b + -1)
            iterations(sp, run)
            store(Batch(BATCHES - 1))
            for i in range(2):
                sp.wait_ge(s_stored[i], 16 * (BATCHES // 2 + 1))

        @block.gpsimd
        def _(pool):
            def gather(b, fresh=False):
                if not fresh:
                    pool.wait_ge(s_h1, done(b + -2, 2, 2))
                nc.gpsimd.tensor_copy(idx_cur[:, b.parity, :], idx_sb[:, bass.ds(b.times(C), C)]).then_inc(s_idxc, 1)
                pool.wait_ge(s_idxc, done(b, 1, 1))
                nc.gpsimd.tensor_tensor(idx_seen[:, :], idx_cur[:, b.parity, :], idx_cur[:, b.parity, :], ALU.add)
                for c in range(C):
                    pool.indirect_dma_start(
                        out=emb[:, b.parity, c, :], out_offset=None, in_=table,
                        in_offset=bass.IndirectOffsetOnAxis(ap=idx_cur[:, b.parity, c:c + 1], axis=0),
                    ).then_inc(s_gather[b.parity], 16)

            def add_bias(b):
                pool.wait_ge(s_h2, done(b, 2, 2))
                pool.wait_ge(s_stored[b.parity], done_parity(b, 16, 16))
                nc.gpsimd.tensor_tensor(outb[:, b.parity, :, :], h2[:, :, :],
                                        bias_sb[:, :].unsqueeze(1).to_broadcast([P, C, D]),
                                        ALU.add).then_inc(s_h2b, 1)

            def norm_rstd(which, b):
                pool.wait_ge(s_mv[which], done(b, 1, 1))
                cols = [cst[:, i:i + 1].to_broadcast([P, C]) for i in (C_EPS, C_POWER)]
                nc.gpsimd.tensor_tensor(ln_ve[which][:, :], ln_mv[which][:, :, 1], cols[0],
                                        ALU.add).then_inc(s_ve[which], 1)
                pool.wait_ge(s_ve[which], done(b, 1, 1))
                nc.gpsimd.tensor_tensor(ln_rstd[which][:, :], ln_ve[which][:, :], cols[1],
                                        ALU.pow).then_inc(s_rstd[which], 1)

            pool.wait_ge(s_idx, 16)
            b0 = Batch(0)
            gather(b0, fresh=True)
            pool.wait_ge(s_small, 16 * SMALL_LOADS)
            pool.wait_ge(s_cst, 16)
            norm_rstd(0, b0)

            def run(b, first, last):
                if not last:
                    gather(b + 1, fresh=first)
                if not first:
                    add_bias(b + -1)
                    norm_rstd(1, b + -1)
                if not last:
                    norm_rstd(0, b + 1)
            iterations(pool, run)
            e = Batch(BATCHES - 1)
            add_bias(e)
            norm_rstd(1, e)

        @block.tensor
        def _(pe):
            def mm(*args, **kw):
                return nc.tensor.matmul(*args, skip_group_check=True, **kw)

            def split_mm(dst, lhs, rhs, slabs):
                n = 0
                for k in range(slabs):
                    for x, w in ((0, 0), (1, 0), (0, 1)):
                        last = mm(dst, lhs(x, k), rhs(w, k), start=(n == 0), stop=(n == 3 * slabs - 1))
                        n += 1
                return last

            def low_rank():
                pe.wait_ge(s_small, 16 * SMALL_LOADS)
                mm(misc[0:4, 0:D], raw_ld[0:100, 0:4], raw_da[0:100, :], start=True, stop=True).then_inc(s_low, 1)
                pe.wait_ge(s_lowc, 1)
                mm(misc[0:50, 0:D], raw_lu[0:4, 0:50], low1[0:4, :], start=True, stop=True).then_inc(s_low, 1)
                pe.wait_ge(s_lowc, 2)
                for k in range(KD):
                    last = mm(misc_pair[:, k, :], low2[0:50, k * P:(k + 1) * P], raw_ua[0:50, :],
                              start=(k == 0), stop=True)
                last.then_inc(s_low, 1)

            def turn(src):
                for c in range(C):
                    last = nc.tensor.transpose(misc[:, c * P:(c + 1) * P], src(c), ident)
                return last

            def turn_a(b):
                pe.wait_ge(s_arep, done(b, 1, 1))
                turn(lambda c: a_rep[:, c, :]).then_inc(s_atp, 1)

            def lora(b, pair):
                if pair == 0:
                    pe.wait_ge(s_ast, done(b, 1, 1))
                else:
                    pe.wait_ge(s_h1, done(b, 2, 1))
                for i in range(2):
                    t = (2 * pair + i) * P
                    last = mm(misc_pair[:, i, :], a_stack[:, t:t + P], lb_stack[:, :], start=(i == 0), stop=True)
                last.then_inc(s_lora, 1)

            def turn_y(which, y, b, pair):
                pe.wait_ge(s_y[which], done(b, 2, pair + 1))
                for i in range(2):
                    for k in range(KD):
                        j = k * 2 + i
                        last = nc.tensor.transpose(misc[:, j * P:(j + 1) * P], y[:, 2 * pair + i, k * P:(k + 1) * P],
                                                   ident)
                last.then_inc(s_ytp[which], 1)

            def qkv(b, first):
                parts = (y1_hi, y1_lo)
                w = (wqkv_hi, wqkv_lo)
                for c in range(C):
                    if c % 2 == 0:
                        pe.wait_ge(s_ylo[0], done(b, 2, c // 2 + 1))
                    for j in range(3):
                        if c > 0:
                            pe.wait_ge(s_vev, done(b, 3 * C, 3 * (c - 1) + j + 1))
                        elif not first and j < 2:
                            pe.wait_ge(s_atlo, done(b + -1, C, 3))
                        elif not first:
                            pe.wait_ge(s_stm, done(b + -1, C - 1, C - 1))
                        split_mm(ps[:, j, 0:THIRD], lambda x, k: parts[x][:, k, c * P:(c + 1) * P],
                                 lambda x, k: w[x][:, k, j * THIRD:(j + 1) * THIRD], KD).then_inc(s_vmm, 1)

            def out_proj(b, c):
                parts, w = (at_hi, at_lo), (wo_hi, wo_lo)
                if c == 0:
                    pe.wait_ge(s_atlo, done(b, C, C))
                last = split_mm(proj_ps[c // 2][:, c % 2, :], lambda x, k: parts[x][:, k, c, :],
                                lambda x, k: w[x][:, k, :], PAIRS)
                if c % 2 == 1:
                    last.then_inc(s_omm, 1)

            def k_sums(b):
                pe.wait_ge(s_fk, done(b, 1, 1))
                mm(misc[:, 0:C * H * FEAT], causal, fk[:, :, :].rearrange("p c n -> p (c n)"), start=True, stop=False)
                n = H * FEAT
                for c in range(C - 1):
                    later = C - 1 - c
                    last = mm(misc[:, (c + 1) * n:C * n].rearrange("p (c n) -> p c n", n=n), ones,
                              fk[:, c, :].unsqueeze(1).to_broadcast([P, later, n]), start=False, stop=(c == C - 2))
                last.then_inc(s_cumk, 1)

            def turn_k(b):
                pe.wait_ge(s_krep, done(b, 1, 1))
                pe.wait_ge(s_prod, done(b, 1, 1))
                turn(lambda c: k_rep[:, c, :]).then_inc(s_ktp, 1)

            def turn_q(b):
                pe.wait_ge(s_qrep, done(b, 1, 1))
                turn(lambda c: q_rep[:, c, :]).then_inc(s_qtp, 1)

            def weights(b, c, g):
                n = c * G + g
                if n == 0:
                    pe.wait_ge(s_kgrp, done(b, 1, 1))
                    pe.wait_ge(s_qhead, done(b, 1, 1))
                if n >= 2:
                    pe.wait_ge(s_wts, done(b, C * G, n - 1))
                mm(ps[:, 5 + n % 2, :].rearrange("p (h t) -> p h t", t=P), k_group[:, g, c * P:(c + 1) * P],
                   q_head[:, :, c * P:(c + 1) * P], start=True, stop=True).then_inc(s_wmm, 1)

            def heads_free(b, c, first):
                if c == 0:
                    pe.wait_ge(s_vev, done(b, 3 * C, 3 * C))
                elif c == 1 and not first:
                    pe.wait_ge(s_h2, done(b + -1, 2, 2))
                elif c >= 2:
                    pe.wait_ge(s_atlo, done(b, C, c - 1))

            def cross(b, c):
                pe.wait_ge(s_st, done(b, C - 1, c))
                if c == 1:
                    pe.wait_ge(s_qgrp, done(b, 1, 1))
                for i in range(PAIRS):
                    mm(heads_ps[c % 2][:, i, :], st[:, (i % 2) * P:(i % 2 + 1) * P],
                       q_group[:, i // 2, c * P:(c + 1) * P], start=(i % 4 == 0), stop=False)

            def state(b, c):
                if c > 0:
                    pe.wait_ge(s_stm, done(b, C - 1, c))
                for g in range(G):
                    last = mm(state_ps[32 * g:32 * (g + 1), :], k_rep[:, c, 32 * g:32 * (g + 1)],
                              V[:, c, g * HG * E:(g + 1) * HG * E], start=(c == 0), stop=True,
                              tile_position=(0, 32 * g))
                last.then_inc(s_stmm, 1)

            def attend(b, c, g):
                pe.wait_ge(s_wts, done(b, C * G, c * G + g + 1))
                for h in range(g * HG, (g + 1) * HG):
                    half = slice(64 * (h % 2), 64 * (h % 2) + 64)
                    opens = c == 0 and h % 8 < 2
                    last = mm(heads_ps[c % 2][half, h // 2, :], V[:, c, h * E:(h + 1) * E], wts[:, c % 2, h, :],
                              start=opens, stop=(h % 8 >= 6))
                last.then_inc(s_at, 1)

            def ffn(b, pair):
                parts, w = (y2_hi, y2_lo), (wff_hi, wff_lo)
                if pair == 0:
                    pe.wait_ge(s_ylo[1], done(b, 2, 2))
                else:
                    pe.wait_ge(s_out, done(b, 2, 1))
                for i in range(2):
                    t = (2 * pair + i) * P
                    last = split_mm(misc_pair[:, i, :], lambda x, k: parts[x][:, k, t:t + P],
                                    lambda x, k: w[x][:, k, :], KD)
                last.then_inc(s_ffmm, 1)

            pe.wait_ge(s_cst, 16)
            low_rank()
            pe.wait_ge(s_wdone, 3)
            b0 = Batch(0)
            turn_a(b0)
            lora(b0, 0)
            lora(b0, 1)
            pe.wait_ge(s_h1, done(b0, 2, 2))
            turn_y(0, y1, b0, 0)
            pe.wait_ge(s_ylo[0], done(b0, 2, 1))
            turn_y(0, y1, b0, 1)

            def slot(b, c, second, first, last):
                if c == 0 and not last:
                    if not second:
                        lora(b + 1, 0)
                    else:
                        lora(b + 1, 1)
                if c == 1 and not first:
                    if not second:
                        pe.wait_ge(s_h1, done(b + 1, 2, 2)) if not last else pe.wait_ge(s_qmix, done(b, 1, 1))
                    else:
                        pe.wait_ge(s_ylo[1], done(b + -1, 2, 1))
                    turn_y(1, y2, b + -1, int(second))
                if c == 2 and not first:
                    ffn(b + -1, int(second))
                if c == 3 and not last:
                    if second:
                        pe.wait_ge(s_ylo[0], done(b + 1, 2, 1))
                    elif not first:
                        pe.wait_ge(s_out, done(b + -1, 2, 2))
                    else:
                        pe.wait_ge(s_h1, done(b + 1, 2, 2))
                    turn_y(0, y1, b + 1, int(second))

            def run(b, first, last):
                qkv(b, first)
                if not first:
                    out_proj(b + -1, 0)
                    out_proj(b + -1, 1)
                pe.wait_ge(s_ylo[0], done(b, 2, 2))
                k_sums(b)
                if not first:
                    out_proj(b + -1, 2)
                turn_k(b)
                if not first:
                    out_proj(b + -1, 3)
                pe.wait_ge(s_kmix, done(b, 1, 1))
                if not last:
                    turn_a(b + 1)
                    pe.wait_ge(s_ast, done(b + 1, 1, 1))
                turn_q(b)
                pe.wait_ge(s_qmix, done(b, 1, 1))
                weights(b, 0, 0)
                weights(b, 0, 1)
                for c in range(C):
                    heads_free(b, c, first)
                    if c > 0:
                        cross(b, c)
                    if c < C - 1:
                        state(b, c)
                    weights(b, c, 2)
                    attend(b, c, 0)
                    weights(b, c, 3)
                    attend(b, c, 1)
                    slot(b, c, False, first, last)
                    if c < C - 1:
                        weights(b, c + 1, 0)
                    attend(b, c, 2)
                    if c < C - 1:
                        weights(b, c + 1, 1)
                    attend(b, c, 3)
                    slot(b, c, True, first, last)
            iterations(pe, run)

            e = Batch(BATCHES - 1)
            for c in range(C):
                out_proj(e, c)
            turn_y(1, y2, e, 0)
            pe.wait_ge(s_ylo[1], done(e, 2, 1))
            turn_y(1, y2, e, 1)
            ffn(e, 0)
            ffn(e, 1)

        @block.scalar
        def _(act):
            def copy(dst, src):
                return nc.scalar.activation(dst, src, ACT.Copy)

            def v_copy(b, c):
                for j in range(3):
                    act.wait_ge(s_vmm, done(b, 3 * C, 3 * c + j + 1))
                    if j < 2:
                        copy(V[:, c, j * THIRD:(j + 1) * THIRD], ps[:, j, 0:THIRD]).then_inc(s_vev, 1)
                    else:
                        copy(V[:, c, 2 * THIRD:HE], ps[:, 2, 0:VLAST])
                        nc.scalar.activation(th[:, c, :], ps[:, 2, VLAST:THIRD], ACT.Tanh).then_inc(s_vev, 1)

            def features(b):
                act.wait_ge(s_vev, done(b, 3 * C, 3 * C))
                if not (b.reg is None and b.fixed == 0):
                    act.wait_ge(s_qrep, done(b + -1, 1, 1))
                for f, ready, o in ((fk, s_fk, H), (fq, s_fq, 0)):
                    pairs = f[:, :, :].rearrange("p c (h f) -> p c h f", f=FEAT)
                    nc.scalar.activation(pairs[:, :, :, 0], th[:, :, o:o + H], ACT.Sin, scale=QUARTER_PI,
                                         bias=cst[:, C_HALFPI:C_HALFPI + 1])
                    nc.scalar.activation(pairs[:, :, :, 1], th[:, :, o:o + H], ACT.Sin,
                                         scale=QUARTER_PI).then_inc(ready, 1)

            def hi_of_misc(turned, ready, mixed_before):
                act.wait_ge(*turned)
                if mixed_before is not None:
                    act.wait_ge(*mixed_before)
                copy(round_hi[:, :], misc).then_inc(ready, 1)

            def k_groups(b):
                act.wait_ge(s_kmix, done(b, 1, 1))
                for g in range(G):
                    rows = slice(32 * g, 32 * (g + 1))
                    last = copy(k_group[rows, g, :], k_mix[rows, :])
                last.then_inc(s_kgrp, 1)

            def q_groups(b):
                act.wait_ge(s_qmix, done(b, 1, 1))
                for g in range(G):
                    rows = slice(32 * g, 32 * (g + 1))
                    last = copy(q_group[rows, g, :], q_mix[rows, :])
                last.then_inc(s_qgrp, 1)

            def y_hi(which, hi, b, pair):
                act.wait_ge(s_ytp[which], done(b, 2, pair + 1))
                copy(hi[:, :, 2 * pair * P:2 * (pair + 1) * P], misc.rearrange("p (k t) -> p k t", k=KD))\
                    .then_inc(s_yhi[which], 1)

            def state_hi(b, c):
                act.wait_ge(s_stm, done(b, C - 1, c + 1))
                copy(st_hi[:, :], st_mask[:, :, :].rearrange("p h e -> p (h e)")).then_inc(s_sthi, 1)

            def heads_hi(b, c):
                act.wait_ge(s_at, done(b, C * G, (c + 1) * G))
                copy(at_hi[:, :, c, :], heads_ps[c % 2]).then_inc(s_athi, 1)

            act.wait_ge(s_cst, 16)
            nc.scalar.activation(rden[:, 0:1], cst[:, 0:1], ACT.Silu)
            act.wait_ge(s_wqkv, 16)
            copy(wqkv_hi[:, :, :], raw_qkv).then_inc(s_whi, 1)
            act.wait_ge(s_wo, 16)
            copy(wo_hi[:, :, :], raw_wo).then_inc(s_whi, 1)
            act.wait_ge(s_low, 1)
            copy(low1[0:4, :], misc[0:4, 0:D]).then_inc(s_lowc, 1)
            act.wait_ge(s_low, 2)
            copy(low2[0:50, :], misc[0:50, 0:D]).then_inc(s_lowc, 1)
            act.wait_ge(s_lb2, 1)
            copy(round_hi[:, 0:D], lb2).then_inc(s_lbhi, 1)
            act.wait_ge(s_wff, 1)
            copy(wff_hi[:, :, :], raw_ff).then_inc(s_whi, 1)
            b0 = Batch(0)
            hi_of_misc((s_atp, 1), s_ahi, (s_wdone, 3))
            y_hi(0, y1_hi, b0, 0)
            y_hi(0, y1_hi, b0, 1)

            def run(b, first, last):
                for c in range(C):
                    v_copy(b, c)
                features(b)
                hi_of_misc((s_ktp, done(b, 1, 1)), s_khi, (s_ast, done(b, 1, 1)))
                k_groups(b)
                if not last:
                    hi_of_misc((s_atp, done(b + 1, 1, 1)), s_ahi, (s_kmix, done(b, 1, 1)))
                hi_of_misc((s_qtp, done(b, 1, 1)), s_qhi, (s_ast, done(b + 1, 1, 1)) if not last else None)
                q_groups(b)
                for c in range(C):
                    if c < C - 1:
                        state_hi(b, c)
                    if c == 1 and not first:
                        y_hi(1, y2_hi, b + -1, 0)
                    if c == 3 and not last:
                        y_hi(0, y1_hi, b + 1, 0)
                    heads_hi(b, c)
                    if c == 1 and not first:
                        y_hi(1, y2_hi, b + -1, 1)
                    if c == 3 and not last:
                        y_hi(0, y1_hi, b + 1, 1)
            iterations(act, run)
            e = Batch(BATCHES - 1)
            y_hi(1, y2_hi, e, 0)
            y_hi(1, y2_hi, e, 1)

        @block.vector
        def _(dve):
            tt = nc.vector.tensor_tensor

            def stack(dst, hi, whole, lo_rows):
                return nc.vector.scalar_tensor_tensor(dst, hi.bitcast(F32), lo_rows, whole, ALU.mult, ALU.add)

            def a_copies(b):
                dve.wait_ge(s_gather[b.parity], done_parity(b, 16 * C, 16 * C))
                if not (b.reg is None and b.fixed == 0):
                    dve.wait_ge(s_atp, done(b + -1, 1, 1))
                nc.vector.tensor_copy(
                    a_rep[:, :, 0:COPIES * R].rearrange("p c (n r) -> p c n r", r=R),
                    emb[:, b.parity, :, D:ROW].unsqueeze(2).to_broadcast([P, C, COPIES, R])).then_inc(s_arep, 1)

            def a_to_stack(b):
                dve.wait_ge(s_ahi, done(b, 1, 1))
                stack(a_stack[:, :], round_hi[:, :], misc, lo_k).then_inc(s_ast, 1)

            def add_lora(b, pair):
                dve.wait_ge(s_lora, done(b, 2, pair + 1))
                tt(h1[:, b.parity, 2 * pair:2 * pair + 2, :], emb[:, b.parity, 2 * pair:2 * pair + 2, 0:D],
                   misc_pair, ALU.add).then_inc(s_h1, 1)

            def norm_stats(which, x, ready, b):
                dve.wait_ge(*ready)
                for c in range(C):
                    last = nc.vector.bn_stats(ln[which][:, c, :], x[:, c, :])
                last.then_inc(s_stats[which], 1)
                dve.wait_ge(s_cst, 16)
                dve.wait_ge(s_stats[which], done(b, 1, 1))
                for c in range(C):
                    last = nc.vector.bn_aggr(ln_mv[which][:, c, :], ln[which][:, c, :])
                last.then_inc(s_mv[which], 1)

            def norm_apply(which, x, y, b):
                dve.wait_ge(s_rstd[which], done(b, 1, 1))
                if not (b.reg is None and b.fixed == 0):
                    dve.wait_ge(s_ytp[which], done(b + -1, 2, 2))
                for c in range(C):
                    last = nc.vector.tensor_scalar(y[:, c, :], x[:, c, :], ln_mv[which][:, c, 0:1],
                                                   ln_rstd[which][:, c:c + 1], ALU.subtract, ALU.mult)
                    if c % 2 == 1:
                        last.then_inc(s_y[which], 1)

            def y_lo(which, hi, lo, b, pair):
                dve.wait_ge(s_yhi[which], done(b, 2, pair + 1))
                t = slice(2 * pair * P, 2 * (pair + 1) * P)
                tt(lo[:, :, t], misc.rearrange("p (k t) -> p k t", k=KD), hi[:, :, t].bitcast(F32),
                   ALU.subtract).then_inc(s_ylo[which], 1)

            def k_copies(b):
                dve.wait_ge(s_fk, done(b, 1, 1))
                nc.vector.tensor_copy(
                    k_rep[:, :, :].rearrange("p c (g n x) -> p (c g) n x", g=G, n=COPIES),
                    fk[:, :, :].rearrange("p c (g x) -> p (c g) x", g=G).unsqueeze(2)
                    .to_broadcast([P, C * G, COPIES, HG * FEAT])).then_inc(s_krep, 1)

            def q_over_den(b):
                dve.wait_ge(s_fq, done(b, 1, 1))
                dve.wait_ge(s_cumk, done(b, 1, 1))
                flat = lambda x: x[:, :, :].rearrange("p c n -> p (c n)")
                tt(flat(prod), flat(fq), misc[:, 0:C * H * FEAT], ALU.mult).then_inc(s_prod, 1)
                dve.wait_ge(s_prod, done(b, 1, 1))
                pairs = flat(prod).rearrange("p (n f) -> p n f", f=FEAT)
                nc.vector.scalar_tensor_tensor(den[:, :], pairs[:, :, 0], DEN_EPS, pairs[:, :, 1], ALU.add,
                                               ALU.add).then_inc(s_den, 1)
                dve.wait_ge(s_den, done(b, 1, 1))
                nc.vector.reciprocal(rden[:, :], den[:, :]).then_inc(s_rden, 1)
                dve.wait_ge(s_rden, done(b, 1, 1))
                tt(flat(fqn).rearrange("p (n f) -> p n f", f=FEAT), flat(fq).rearrange("p (n f) -> p n f", f=FEAT),
                   rden[:, :].unsqueeze(2).to_broadcast([P, C * H, FEAT]), ALU.mult).then_inc(s_fqn, 1)
                dve.wait_ge(s_fqn, done(b, 1, 1))
                nc.vector.tensor_copy(
                    q_rep[:, :, :].rearrange("p c (g n x) -> p (c g) n x", g=G, n=COPIES),
                    fqn[:, :, :].rearrange("p c (g x) -> p (c g) x", g=G).unsqueeze(2)
                    .to_broadcast([P, C * G, COPIES, HG * FEAT])).then_inc(s_qrep, 1)

            def k_to_mix(b, first):
                dve.wait_ge(s_khi, done(b, 1, 1))
                if not first:
                    dve.wait_ge(s_kgrp, done(b + -1, 1, 1))
                stack(k_mix[:, :], round_hi[:, :], misc, lo_k).then_inc(s_kmix, 1)

            def q_to_mix(b, first):
                dve.wait_ge(s_qhi, done(b, 1, 1))
                if not first:
                    dve.wait_ge(s_qgrp, done(b + -1, 1, 1))
                stack(q_mix[:, :], round_hi[:, :], misc, lo_q).then_inc(s_qmix, 1)

            def q_heads(b):
                dve.wait_ge(s_qmix, done(b, 1, 1))
                for h in range(HG):
                    last = nc.vector.tensor_scalar(q_head[:, h, :], q_mix[:, :], cst[:, C_HEAD + h:C_HEAD + h + 1],
                                                   None, ALU.mult)
                last.then_inc(s_qhead, 1)

            def add_attention(b, pair):
                dve.wait_ge(s_omm, done(b, 2, pair + 1))
                if pair == 0 and not (b.reg is None and b.fixed == 0):
                    dve.wait_ge(s_h2b, done(b + -1, 1, 1))
                tt(h2[:, 2 * pair:2 * pair + 2, :], h1[:, b.parity, 2 * pair:2 * pair + 2, :], proj_ps[pair],
                   ALU.add).then_inc(s_h2, 1)

            def mask(b, c, g):
                n = c * G + g
                dve.wait_ge(s_wmm, done(b, C * G, n + 1))
                if c >= 2:
                    dve.wait_ge(s_at, done(b, C * G, n - 2 * G + 1))
                tt(wts[:, c % 2, g * HG:(g + 1) * HG, :], ps[:, 5 + n % 2, :].rearrange("p (h t) -> p h t", t=P),
                   causal.unsqueeze(1).to_broadcast([P, HG, P]), ALU.mult).then_inc(s_wts, 1)

            def mask_state(b, c):
                dve.wait_ge(s_stmm, done(b, C - 1, c + 1))
                tt(st_mask[:, :, :], state_ps.rearrange("p (h e) -> p h e", e=E),
                   cst[:, C_HEAD:C_HEAD + HG].unsqueeze(2).to_broadcast([P, HG, E]), ALU.mult).then_inc(s_stm, 1)

            def state_to_stack(b, c):
                dve.wait_ge(s_sthi, done(b, C - 1, c + 1))
                stack(st[:, :], st_hi[:, :], st_mask[:, :, :].rearrange("p h e -> p (h e)"), lo_k).then_inc(s_st, 1)

            def heads_lo(b, c):
                dve.wait_ge(s_athi, done(b, C, c + 1))
                tt(at_lo[:, :, c, :], heads_ps[c % 2], at_hi[:, :, c, :].bitcast(F32), ALU.subtract)\
                    .then_inc(s_atlo, 1)

            def add_ffn(b, pair):
                dve.wait_ge(s_ffmm, done(b, 2, pair + 1))
                if pair == 0:
                    dve.wait_ge(s_h2b, done(b, 1, 1))
                o = outb[:, b.parity, 2 * pair:2 * pair + 2, :]
                tt(o, o, misc_pair, ALU.add).then_inc(s_out, 1)

            nc.vector.memset(h2[:, :, :], 0.0).then_inc(s_zero, 1)
            for x in (a_rep, k_group, q_group):
                z = x[:, :, :]
                nc.vector.memset(z.bitcast(F32) if x is not a_rep else z, 0.0)
            b0 = Batch(0)
            dve.wait_ge(s_cst, 16)
            dve.wait_ge(s_small, 16 * SMALL_LOADS)
            nc.vector.tensor_scalar(lb2, raw_lb, LORA_SCALE, None, ALU.mult).then_inc(s_lb2, 1)
            dve.wait_ge(s_low, 3)
            tt(raw_ff, raw_ff, misc_pair, ALU.add).then_inc(s_wff, 1)
            dve.wait_ge(s_lbhi, 1)
            stack(lb_stack[:, :], round_hi[:, 0:D], lb2, lo_q).then_inc(s_lbs, 1)
            for n, (lo, whole, hi) in enumerate(((wqkv_lo, raw_qkv, wqkv_hi), (wo_lo, raw_wo, wo_hi),
                                                 (wff_lo, raw_ff, wff_hi))):
                dve.wait_ge(s_whi, n + 1)
                tt(lo[:, :, :], whole, hi[:, :, :].bitcast(F32), ALU.subtract).then_inc(s_wdone, 1)
            a_copies(b0)
            a_to_stack(b0)
            add_lora(b0, 0)
            add_lora(b0, 1)
            norm_stats(0, h1[:, 0, :, :], (s_h1, 2), b0)
            norm_apply(0, h1[:, 0, :, :], y1, b0)
            y_lo(0, y1_hi, y1_lo, b0, 0)
            y_lo(0, y1_hi, y1_lo, b0, 1)

            def run(b, first, last):
                prev, nxt = b + -1, b + 1
                if not last:
                    a_copies(nxt)
                if not first:
                    add_attention(prev, 0)
                k_copies(b)
                q_over_den(b)
                k_to_mix(b, first)
                if not last:
                    a_to_stack(nxt)
                if not first:
                    add_attention(prev, 1)
                q_to_mix(b, first)
                q_heads(b)
                for c in range(C):
                    mask(b, c, 0)
                    mask(b, c, 1)
                    if c < C - 1:
                        mask_state(b, c)
                    if c > 0:
                        heads_lo(b, c - 1)
                    if c == 0 and not first:
                        norm_stats(1, h2, (s_h2, done(prev, 2, 2)), prev)
                    if c == 1 and not last:
                        add_lora(nxt, 1)
                    if c == 2 and not first:
                        y_lo(1, y2_hi, y2_lo, prev, 1)
                    if c == 3 and not first:
                        add_ffn(prev, 1)
                    mask(b, c, 2)
                    if c < C - 1:
                        state_to_stack(b, c)
                    mask(b, c, 3)
                    if c == 0 and not last:
                        add_lora(nxt, 0)
                    if c == 0 and not first:
                        norm_apply(1, h2, y2, prev)
                    if c == 1 and not first:
                        y_lo(1, y2_hi, y2_lo, prev, 0)
                    if c == 1 and not last:
                        norm_stats(0, h1[:, nxt.parity, :, :], (s_h1, done(nxt, 2, 2)), nxt)
                    if c == 2 and not first:
                        add_ffn(prev, 0)
                    if c == 2 and not last:
                        norm_apply(0, h1[:, nxt.parity, :, :], y1, nxt)
                    if c == 3 and not last:
                        y_lo(0, y1_hi, y1_lo, nxt, 0)
                heads_lo(b, C - 1)
                if not last:
                    y_lo(0, y1_hi, y1_lo, nxt, 1)
            iterations(dve, run)

            e = Batch(BATCHES - 1)
            add_attention(e, 0)
            add_attention(e, 1)
            norm_stats(1, h2, (s_h2, done(e, 2, 2)), e)
            norm_apply(1, h2, y2, e)
            y_lo(1, y2_hi, y2_lo, e, 0)
            y_lo(1, y2_hi, y2_lo, e, 1)
            add_ffn(e, 0)
            add_ffn(e, 1)


def constants():
    import numpy as np
    a = np.zeros((P, N_CONST), np.float32)
    row = np.arange(P)
    a[:, C_CAUSAL:C_CAUSAL + P] = row[:, None] <= row[None, :]
    a[:, C_ONES:C_ONES + P] = 1
    a[:, C_IDENT:C_IDENT + P] = np.eye(P)
    copy = row // (HG * FEAT) % COPIES
    a[:, C_LO_K] = -1.0 * (copy >= 2)
    a[:, C_LO_Q] = -1.0 * (copy % 2)
    for h in range(HG):
        a[:, C_HEAD + h] = row // FEAT % HG == h
    a[:, C_HALFPI] = np.pi / 2
    a[:, C_EPS] = LN_EPS
    a[:, C_POWER] = -0.5
    return a


def kernel(x, L0_tok_W, L0_tok_lora_A, L0_tok_lora_B, L0_attn_W_Q, L0_attn_W_K, L0_attn_W_V, L0_attn_W_O,
           L0_ffn_W, L0_ffn_b, L0_ffn_lora_down, L0_ffn_lora_up, L0_ffn_down_aux, L0_ffn_up_aux):
    import numpy as np
    import concourse.bacc as bacc
    from concourse.bass_utils import run_bass_kernel_spmd

    layout = {
        "idx": np.asarray(x).reshape(BATCHES * C, P).T,
        "table": np.concatenate([np.asarray(L0_tok_W), np.asarray(L0_tok_lora_A).T], axis=1),
        "wqkv": np.concatenate([np.asarray(L0_attn_W_V).transpose(1, 0, 2).reshape(D, HE),
                                np.asarray(L0_attn_W_Q)[:, :, 0].T, np.asarray(L0_attn_W_K)[:, :, 0].T], axis=1),
        "wo": np.asarray(L0_attn_W_O).transpose(2, 1, 0).reshape(HE, D),
        "wff": np.asarray(L0_ffn_W).T,
        "ld_t": np.asarray(L0_ffn_lora_down).T,
        "lu_t": np.asarray(L0_ffn_lora_up).T,
        "da": np.asarray(L0_ffn_down_aux),
        "ua_t": np.asarray(L0_ffn_up_aux).T,
        "lb_t": np.asarray(L0_tok_lora_B).T,
        "bias": np.asarray(L0_ffn_b),
        "consts": constants(),
    }
    nc = bacc.Bacc("TRN2", target_bir_lowering=False, num_devices=1)
    arrays, args = {}, []
    for name, a in layout.items():
        a = np.ascontiguousarray(a)
        arrays[f"in_{name}"] = a
        args.append(nc.dram_tensor(f"in_{name}", a.shape, mybir.dt.from_np(a.dtype), kind="ExternalInput").ap())
    args.append(nc.dram_tensor("out_h", (BATCHES * T, D), F32, kind="ExternalOutput").ap())
    tower(nc, *args)
    r = run_bass_kernel_spmd(nc, [arrays], core_ids=[0])
    return r.results[0]["out_h"].reshape(BATCHES, T, D)
```

```python
from contextlib import ExitStack

import concourse.bass as bass
from concourse import mybir

F32 = mybir.dt.float32
F32R = mybir.dt.float32r
I32 = mybir.dt.int32
ALU = mybir.AluOpType
ACT = mybir.ActivationFunctionType

P = 128
BATCHES = 8
C = 4
T = C * P
D = 256
KD = D // P
H = 16
E = 64
HE = H * E
PAIRS = HE // P
G = 4
HG = H // G
FEAT = 2
R = 8
COPIES = 4
QKV = HE + 2 * H
THIRD = QKV // 3
VLAST = HE - 2 * THIRD
ROW = D + R
LN_EPS = 1e-5
DEN_EPS = 1e-6
LORA_SCALE = 16.0 / 8.0
QUARTER_PI = 3.141592653589793 / 4

FACTORS = 4
N_THIRDS = 3 * C

C_CAUSAL, C_ONES, C_IDENT = 0, P, 2 * P
C_LO_K, C_LO_Q, C_HEAD, C_HALFPI = 3 * P, 3 * P + 1, 3 * P + 2, 3 * P + 2 + HG
C_EPS, C_POWER, C_TILE = C_HALFPI + 1, C_HALFPI + 2, C_HALFPI + 3
N_CONST = C_TILE + C


AHEAD = [(0, 3), (1, 1), (1, 2), (1, 3), (2, 1), (2, 2), (2, 3), (3, 1), (3, 3)]


class Batch:

    def __init__(self, fixed, reg=None):
        self.fixed, self.reg = fixed, reg
        self.parity = fixed % 2

    def __add__(self, n):
        return Batch(self.fixed + n, self.reg)

    def times(self, n, k=0):
        v = self.fixed * n + k
        return v if self.reg is None else self.reg * (2 * n) + v


def third(b, n):
    if b.reg is None and b.fixed == 0:
        return (n, 2) if n < C else ((n - C) // 2, (n - C) % 2)
    return n // 3, n % 3


def done(b, per, k):
    return b.times(per, k)


def done_parity(b, per, k):
    v = (b.fixed // 2) * per + k
    return v if b.reg is None else b.reg * per + v


def tower(nc, idx, table, wqkv, wo, wff, ld_t, lu_t, da, ua_t, lb_t, bias, consts, out):
    with ExitStack() as ctx:
        def sb(name, shape, dt=F32):
            return ctx.enter_context(nc.sbuf_tensor(name, shape, dt))

        def sem(name):
            return ctx.enter_context(nc.semaphore(name))

        cst = sb("cst", [P, N_CONST])
        causal, ones, ident = (cst[:, o:o + P] for o in (C_CAUSAL, C_ONES, C_IDENT))
        lo_k, lo_q = cst[:, C_LO_K:C_LO_K + 1], cst[:, C_LO_Q:C_LO_Q + 1]
        idx_sb = sb("idx_sb", [P, BATCHES * C], I32)
        idx_cur = sb("idx_cur", [P, 2, C], I32)
        idx_seen = sb("idx_seen", [P, C], I32)
        wqkv_hi, wqkv_lo = (sb(f"wqkv_{n}", [P, KD, QKV], F32R) for n in ("hi", "lo"))
        wo_hi, wo_lo = (sb(f"wo_{n}", [P, PAIRS, D], F32R) for n in ("hi", "lo"))
        wff_hi, wff_lo = (sb(f"wff_{n}", [P, KD, D], F32R) for n in ("hi", "lo"))
        lb_tiles = sb("lb_tiles", [P, C, D], F32R)
        bias_sb = sb("bias_sb", [P, D])
        emb = sb("emb", [P, 2, C, ROW])
        a_rep = sb("a_rep", [P, C * COPIES * R])
        a_stack = sb("a_stack", [P, P], F32R)
        h1 = sb("h1", [P, 2, C, D])
        h2 = sb("h2", [P, C, D])
        y1, y2 = sb("y1", [P, C, D]), sb("y2", [P, C, D])
        y1_hi, y1_lo = (sb(f"y1_{n}", [P, KD, T], F32R) for n in ("hi", "lo"))
        y2_hi, y2_lo = (sb(f"y2_{n}", [P, KD, T], F32R) for n in ("hi", "lo"))
        ln = [sb(f"ln{i}", [P, C, 6]) for i in (1, 2)]
        ln_mv = [sb(f"ln_mv{i}", [P, C, 2]) for i in (1, 2)]
        ln_ve = [sb(f"ln_ve{i}", [P, C]) for i in (1, 2)]
        ln_rstd = [sb(f"ln_rstd{i}", [P, C]) for i in (1, 2)]
        V = sb("V", [P, C, HE])
        th = sb("th", [P, C, 2 * H])
        fq, fk = sb("fq", [P, C, H * FEAT]), sb("fk", [P, C, H * FEAT])
        prod = sb("prod", [P, C, H * FEAT])
        den, rden = sb("den", [P, C * H]), sb("rden", [P, C * H])
        fqn = sb("fqn", [P, C, H * FEAT])
        k_rep, q_rep = sb("k_rep", [P, C, P]), sb("q_rep", [P, C, P])
        round_hi = sb("round_hi", [P, T], F32R)
        k_mix, q_mix = sb("k_mix", [P, T]), sb("q_mix", [P, T])
        k_group = sb("k_group", [P, G, T], F32R)
        q_group = sb("q_group", [P, G, T], F32R)
        q_head = sb("q_head", [P, HG, T], F32R)
        wts = sb("wts", [P, 2, H, P])
        st_mask = sb("st_mask", [P, HG, E])
        st_hi = sb("st_hi", [P, HG * E], F32R)
        st = sb("st", [P, HG * E], F32R)
        at_hi, at_lo = (sb(f"at_{n}", [P, PAIRS, C, P], F32R) for n in ("hi", "lo"))
        outb = sb("outb", [P, 2, C, D])
        raw_qkv = V[:, :, :].rearrange("p c n -> p (c n)")[:, 0:KD * QKV].rearrange("p (k n) -> p k n", k=KD)
        raw_wo = outb[:, :, :, :].rearrange("p a c n -> p (a c) n")
        raw_ff = sb("raw_ff", [P, KD, D])[:, :, :]
        raw_da, raw_ua, raw_ld, raw_lu = (h2[:, i, :] for i in range(4))
        raw_lb, low1, low2, lb2 = (y2[:, i, :] for i in range(4))
        lb_all = y1[:, 0, :]

        ps = ctx.enter_context(nc.psum_tensor("ps", [P, 8, 512], F32))
        heads_ps = ps[:, 0:2, :].rearrange("p a (b t) -> p (a b) t", t=P)
        proj_ps = [ps[:, 4 - i, :].rearrange("p (c n) -> p c n", n=D) for i in range(2)]

        def third_ps(n):
            return ps[:, 3 + (1 + n) % 2, 0:THIRD]
        state_ps = ps[:, 2, 0:HG * E]
        sums_ps = ps[:, 2, HG * E:HG * E + C * H * FEAT]
        qt_ps, kt_ps = ps[:, 5, :], ps[:, 6, :]
        misc = ps[:, 7, :]
        misc_pair = misc.rearrange("p (c n) -> p c n", n=D)

        s_cst, s_idx, s_wqkv, s_wo, s_lb, s_factors, s_ff, s_bias = (
            sem(n) for n in ("cst_loaded", "idx_loaded", "wqkv_loaded", "wo_loaded", "lora_b_loaded",
                             "low_rank_loaded", "wff_loaded", "bias_loaded"))
        s_gzero, s_low, s_whi, s_wdone, s_lb2, s_lbhi = (
            sem(n) for n in ("group_zeros_ready", "low_rank_mm", "w_hi_ready", "w_ready", "lb2_ready", "lb_hi_ready"))
        s_lowc, s_wff, s_lball, s_lbs = (
            sem(n) for n in ("low_rank_copied", "wff_whole", "lb_stack_ready", "lb_tiles_ready"))
        s_idxc = sem("idx_copied")
        s_gather = [sem(f"gathered{i}") for i in range(2)]
        s_arep, s_atp, s_ahi, s_ast, s_lora, s_h1 = (
            sem(n) for n in ("a_rep_ready", "a_turned", "a_hi_ready", "a_stack_ready", "lora_mm", "h1_ready"))
        s_stats = [sem(f"ln{i}_stats") for i in (1, 2)]
        s_mv = [sem(f"ln{i}_mean_var") for i in (1, 2)]
        s_ve = [sem(f"ln{i}_var_eps") for i in (1, 2)]
        s_rstd = [sem(f"ln{i}_rstd") for i in (1, 2)]
        s_y = [sem(f"y{i}_ready") for i in (1, 2)]
        s_ytp = [sem(f"y{i}_turned") for i in (1, 2)]
        s_yhi = [sem(f"y{i}_hi_ready") for i in (1, 2)]
        s_ylo = [sem(f"y{i}_lo_ready") for i in (1, 2)]
        s_vmm, s_vev, s_fk, s_fq, s_cumk = (
            sem(n) for n in ("qkv_mm", "qkv_copied", "k_features", "q_features", "k_sums_mm"))
        s_krep, s_prod, s_den, s_rden, s_fqn, s_qrep = (
            sem(n) for n in ("k_rep_ready", "den_products", "den_ready", "rden_ready", "fqn_ready", "q_rep_ready"))
        s_ktp, s_khi, s_kmix, s_kgrp = (sem(n) for n in ("k_turned", "k_hi_ready", "k_mix_ready", "k_group_ready"))
        s_qtp, s_qhi, s_qmix, s_qhead, s_qgrp = (
            sem(n) for n in ("q_turned", "q_hi_ready", "q_mix_ready", "q_head_ready", "q_group_ready"))
        s_wmm, s_wts, s_at = sem("weights_mm"), sem("weights_masked"), sem("attention_mm")
        s_stmm, s_stm, s_sthi, s_st = (
            sem(n) for n in ("state_mm", "state_masked", "state_hi_ready", "state_ready"))
        s_athi, s_atlo = sem("at_hi_ready"), sem("at_lo_ready")
        s_keep = sem("h1_kept")
        s_omm, s_h2, s_h2b, s_ffmm, s_out = (
            sem(n) for n in ("proj_mm", "h2_ready", "h2_bias_added", "ffn_mm", "out_ready"))
        s_stored = [sem(f"stored{i}") for i in range(2)]

        def iterations(eng, run):
            run(Batch(0), True, False)
            with eng.Fori(0, (BATCHES - 2) // 2) as i:
                run(Batch(1, i), False, False)
                run(Batch(2, i), False, False)
            run(Batch(BATCHES - 1), False, True)

        def added(b, pairs):
            return done(b, 2, pairs + 2)

        block = ctx.enter_context(nc.Block())

        @block.sync
        def _(sp):
            for i in range(2):
                sp.sem_inc(s_stored[i], 16)
            sp.dma_start(idx_sb[:, :], idx).then_inc(s_idx, 16)
            for dst, src in ((raw_ld, ld_t), (raw_da, da), (raw_lu, lu_t), (raw_ua, ua_t)):
                sp.dma_start(dst[0:src.shape[0], 0:src.shape[1]], src).then_inc(s_factors, 16)
            sp.dma_start(raw_lb, lb_t).then_inc(s_lb, 16)
            sp.dma_start(raw_ff, wff.rearrange("(k p) n -> p k n", p=P)).then_inc(s_ff, 16)
            sp.dma_start(bias_sb[:, :], bias.partition_broadcast(P)).then_inc(s_bias, 16)
            sp.wait_ge(s_gather[0], 16 * C)
            sp.dma_start(raw_wo, wo.rearrange("(k p) n -> p k n", p=P)).then_inc(s_wo, 16)

            def store(b):
                sp.wait_ge(s_out, added(b, 2))
                rows = out[bass.ds(b.times(T), T), :].rearrange("(c p) n -> p c n", p=P)
                sp.dma_start(rows, outb[:, b.parity, :, :]).then_inc(s_stored[b.parity], 16)

            def run(b, first, last):
                if not first:
                    store(b + -1)
            iterations(sp, run)
            e = Batch(BATCHES - 1)
            for pair in range(2):
                sp.wait_ge(s_out, added(e, pair + 1))
                first_row = e.fixed * T + 2 * pair * P
                rows = out[first_row:first_row + 2 * P, :].rearrange("(c p) n -> p c n", p=P)
                sp.dma_start(rows, outb[:, e.parity, 2 * pair:2 * pair + 2, :]).then_inc(s_stored[e.parity], 16)
            for i in range(2):
                sp.wait_ge(s_stored[i], 16 * (BATCHES // 2 + 1 + i))

        @block.gpsimd
        def _(pool):
            def gather(b, fresh=False):
                if not fresh:
                    pool.wait_ge(s_h1, done(b + -2, 2, 2))
                nc.gpsimd.tensor_copy(idx_cur[:, b.parity, :], idx_sb[:, bass.ds(b.times(C), C)]).then_inc(s_idxc, 1)
                pool.wait_ge(s_idxc, done(b, 1, 1))
                nc.gpsimd.tensor_tensor(idx_seen[:, :], idx_cur[:, b.parity, :], idx_cur[:, b.parity, :], ALU.add)
                for c in range(C):
                    pool.indirect_dma_start(
                        out=emb[:, b.parity, c, :], out_offset=None, in_=table,
                        in_offset=bass.IndirectOffsetOnAxis(ap=idx_cur[:, b.parity, c:c + 1], axis=0),
                    ).then_inc(s_gather[b.parity], 16)

            def add_bias(b, pair):
                pool.wait_ge(s_h2, done(b, 2, pair + 1))
                if pair == 0:
                    pool.wait_ge(s_stored[b.parity], done_parity(b, 16, 16))
                c = slice(2 * pair, 2 * pair + 2)
                nc.gpsimd.tensor_tensor(outb[:, b.parity, c, :], h2[:, c, :],
                                        bias_sb[:, :].unsqueeze(1).to_broadcast([P, 2, D]),
                                        ALU.add).then_inc(s_h2b, 1)

            def norm_rstd(which, b, pair):
                pool.wait_ge(s_mv[which], done(b, 2, pair + 1))
                c = slice(2 * pair, 2 * pair + 2)
                cols = [cst[:, i:i + 1].to_broadcast([P, 2]) for i in (C_EPS, C_POWER)]
                nc.gpsimd.tensor_tensor(ln_ve[which][:, c], ln_mv[which][:, c, 1], cols[0],
                                        ALU.add).then_inc(s_ve[which], 1)
                pool.wait_ge(s_ve[which], done(b, 2, pair + 1))
                nc.gpsimd.tensor_tensor(ln_rstd[which][:, c], ln_ve[which][:, c], cols[1],
                                        ALU.pow).then_inc(s_rstd[which], 1)

            pool.wait_ge(s_idx, 16)
            b0 = Batch(0)
            gather(b0, fresh=True)
            for x in (k_group, q_group):
                last = nc.gpsimd.memset(x[:, :, :].bitcast(F32), 0.0)
            last.then_inc(s_gzero, 1)
            pool.wait_ge(s_bias, 16)
            pool.wait_ge(s_cst, 16)
            norm_rstd(0, b0, 0)
            norm_rstd(0, b0, 1)

            def run(b, first, last):
                prev, nxt = b + -1, b + 1
                if not last:
                    gather(nxt, fresh=first)
                if not last:
                    norm_rstd(0, nxt, 0)
                    norm_rstd(0, nxt, 1)
                if not first:
                    norm_rstd(1, prev, 0)
                    norm_rstd(1, prev, 1)
                    add_bias(prev, 0)
                    add_bias(prev, 1)
            iterations(pool, run)
            e = Batch(BATCHES - 1)
            for pair in range(2):
                norm_rstd(1, e, pair)
                add_bias(e, pair)

        @block.tensor
        def _(pe):
            def mm(*args, **kw):
                return nc.tensor.matmul(*args, skip_group_check=True, **kw)

            def split_mm(dst, lhs, rhs, slabs):
                n = 0
                for k in range(slabs):
                    for x, w in ((0, 0), (1, 0), (0, 1)):
                        last = mm(dst, lhs(x, k), rhs(w, k), start=(n == 0), stop=(n == 3 * slabs - 1))
                        n += 1
                return last

            def low_rank():
                pe.wait_ge(s_factors, 16 * FACTORS)
                mm(misc[0:4, 0:D], raw_ld[0:100, 0:4], raw_da[0:100, :], start=True, stop=True).then_inc(s_low, 1)
                pe.wait_ge(s_lowc, 1)
                mm(misc[0:50, 0:D], raw_lu[0:4, 0:50], low1[0:4, :], start=True, stop=True).then_inc(s_low, 1)
                pe.wait_ge(s_lowc, 2)
                for k in range(KD):
                    last = mm(misc_pair[:, k, :], low2[0:50, k * P:(k + 1) * P], raw_ua[0:50, :],
                              start=(k == 0), stop=True)
                last.then_inc(s_low, 1)

            def turn(dst, src):
                for c in range(C):
                    last = nc.tensor.transpose(dst[:, c * P:(c + 1) * P], src(c), ident)
                return last

            def turn_a(b):
                pe.wait_ge(s_arep, done(b, 1, 1))
                nc.tensor.transpose(misc[:, 0:P], a_rep[:, :], ident).then_inc(s_atp, 1)

            def lora(b, pair):
                pe.wait_ge(s_ast, done(b, 1, 1))
                for i in range(2):
                    last = mm(misc_pair[:, i, :], a_stack[:, :], lb_tiles[:, 2 * pair + i, :], start=(i == 0),
                              stop=True)
                last.then_inc(s_lora, 1)

            def turn_y(which, y, b, pair):
                pe.wait_ge(s_y[which], done(b, 2, pair + 1))
                for i in range(2):
                    for k in range(KD):
                        j = k * 2 + i
                        last = nc.tensor.transpose(misc[:, j * P:(j + 1) * P], y[:, 2 * pair + i, k * P:(k + 1) * P],
                                                   ident)
                last.then_inc(s_ytp[which], 1)

            def qkv(b, n):
                parts, w = (y1_hi, y1_lo), (wqkv_hi, wqkv_lo)
                c, j = third(b, n)
                if n == 0 or (c, third(b, n - 1)[0]) == (2, 1):
                    pe.wait_ge(s_ylo[0], done(b, 2, c // 2 + 1))
                if n >= 2:
                    pe.wait_ge(s_vev, done(b, N_THIRDS, n - 1))
                elif b.reg is None and b.fixed == 1:
                    pe.wait_ge(s_vev, done(b + -1, N_THIRDS, N_THIRDS - 1 + n))
                elif b.reg is not None or b.fixed > 0:
                    pe.wait_ge(s_h2, done(b + -2, 2, n + 1))
                split_mm(third_ps(n), lambda x, k: parts[x][:, k, c * P:(c + 1) * P],
                         lambda x, k: w[x][:, k, j * THIRD:(j + 1) * THIRD], KD).then_inc(s_vmm, 1)

            def out_proj(b, c, halves=(0, 1)):
                if b.reg is None and b.fixed == 0 and c == 0:
                    pe.wait_ge(s_wdone, 3)
                parts, w = (at_hi, at_lo), (wo_hi, wo_lo)
                dst = proj_ps[c // 2][:, c % 2, :]
                for half in halves:
                    pe.wait_ge(s_atlo, done(b, 2 * C, 2 * c + half + 1))
                    if c % 2 == 0 and half == 0:
                        if b.reg is not None or b.fixed < BATCHES - 1:
                            pe.wait_ge(s_vev, done(b + 1, N_THIRDS, N_THIRDS - 1 + c // 2))
                        else:
                            pe.wait_ge(s_h2, done(b + -1, 2, c // 2 + 1))
                    slabs = PAIRS // 2
                    for k in range(half * slabs, (half + 1) * slabs):
                        for x, v in ((0, 0), (1, 0), (0, 1)):
                            last = mm(dst, parts[x][:, k, c, :], w[v][:, k, :], start=(k == 0 and x + v == 0),
                                      stop=(k == PAIRS - 1 and v == 1))
                    if c % 2 == 1 and half == 1:
                        last.then_inc(s_omm, 1)

            def k_sums(b):
                pe.wait_ge(s_fk, done(b, 1, 1))
                mm(sums_ps, causal, fk[:, :, :].rearrange("p c n -> p (c n)"), start=True, stop=False)
                n = H * FEAT
                for c in range(C - 1):
                    later = C - 1 - c
                    last = mm(sums_ps[:, (c + 1) * n:C * n].rearrange("p (c n) -> p c n", n=n), ones,
                              fk[:, c, :].unsqueeze(1).to_broadcast([P, later, n]), start=False, stop=(c == C - 2))
                last.then_inc(s_cumk, 1)

            def turn_k(b):
                pe.wait_ge(s_krep, done(b, 1, 1))
                turn(kt_ps, lambda c: k_rep[:, c, :]).then_inc(s_ktp, 1)

            def turn_q(b):
                pe.wait_ge(s_qrep, done(b, 1, 1))
                turn(qt_ps, lambda c: q_rep[:, c, :]).then_inc(s_qtp, 1)

            def weights(b, c, g):
                n = c * G + g
                if n == 0:
                    pe.wait_ge(s_kgrp, done(b, 1, 1))
                    pe.wait_ge(s_qhead, done(b, 1, 1))
                if n >= 2:
                    pe.wait_ge(s_wts, done(b, C * G, n - 1))
                mm(ps[:, 5 + n % 2, :].rearrange("p (h t) -> p h t", t=P), k_group[:, g, c * P:(c + 1) * P],
                   q_head[:, :, c * P:(c + 1) * P], start=True, stop=True).then_inc(s_wmm, 1)

            def cross(b, c, half):
                if c > 0:
                    pe.wait_ge(s_atlo, done(b, 2 * C, 2 * c - 1 + half))
                    if half == 0:
                        pe.wait_ge(s_st, done(b, C - 1, c))
                    if (c, half) == (1, 0):
                        pe.wait_ge(s_qgrp, done(b, 1, 1))
                    for i in range(4 * half, 4 * half + 4):
                        mm(heads_ps[:, i, :], st[:, (i % 2) * P:(i % 2 + 1) * P],
                           q_group[:, i // 2, c * P:(c + 1) * P], start=(i % 4 == 0), stop=False)
                elif b.reg is not None or b.fixed > 0:
                    pe.wait_ge(s_atlo, done(b + -1, 2 * C, 2 * C - 1 + half))

            def state(b, c):
                if c > 0:
                    pe.wait_ge(s_stm, done(b, C - 1, c))
                for g in range(G):
                    last = mm(state_ps[32 * g:32 * (g + 1), :], k_rep[:, c, 32 * g:32 * (g + 1)],
                              V[:, c, g * HG * E:(g + 1) * HG * E], start=(c == 0), stop=True,
                              tile_position=(0, 32 * g))
                last.then_inc(s_stmm, 1)

            def attend(b, c, g):
                pe.wait_ge(s_wts, done(b, C * G, c * G + g + 1))
                if b.reg is None and b.fixed == 0 and g == 0:
                    pe.wait_ge(s_vev, C + 2 * (c + 1))
                for h in range(g * HG, (g + 1) * HG):
                    half = slice(64 * (h % 2), 64 * (h % 2) + 64)
                    opens = c == 0 and h % 8 < 2
                    last = mm(heads_ps[half, h // 2, :], V[:, c, h * E:(h + 1) * E], wts[:, c % 2, h, :],
                              start=opens, stop=(h % 8 >= 6))
                last.then_inc(s_at, 1)

            def ffn(b, pair):
                parts, w = (y2_hi, y2_lo), (wff_hi, wff_lo)
                pe.wait_ge(s_ylo[1], done(b, 2, pair + 1))
                for i in range(2):
                    t = (2 * pair + i) * P
                    last = split_mm(misc_pair[:, i, :], lambda x, k: parts[x][:, k, t:t + P],
                                    lambda x, k: w[x][:, k, :], KD)
                last.then_inc(s_ffmm, 1)

            misc_read = []

            def with_misc(step, *args, until):
                if misc_read:
                    pe.wait_ge(*misc_read.pop())
                step(*args)
                misc_read.append(until)

            def do_turn_a(b):
                with_misc(turn_a, b, until=(s_ast, done(b, 1, 1)))

            def do_lora(b, pair):
                with_misc(lora, b, pair, until=(s_h1, done(b, 2, pair + 1)))

            def do_turn_y(which, y, b, pair):
                with_misc(turn_y, which, y, b, pair, until=(s_ylo[which], done(b, 2, pair + 1)))

            def do_ffn(b, pair):
                with_misc(ffn, b, pair, until=(s_out, added(b, pair + 1)))

            with_misc(low_rank, until=(s_wff, 1))
            pe.wait_ge(s_cst, 16)
            b0 = Batch(0)
            do_turn_a(b0)
            pe.wait_ge(s_lbs, 1)
            for pair in range(2):
                do_lora(b0, pair)
            do_turn_y(0, y1, b0, 0)
            pe.wait_ge(s_wdone, 1)
            qkv(b0, 0)
            do_turn_y(0, y1, b0, 1)
            for n in range(1, C):
                qkv(b0, n)

            def between(b, c, g, first, last):
                prev, nxt = b + -1, b + 1
                if not last and (c, g) == (0, 1):
                    do_turn_y(0, y1, nxt, 0)
                if not last and (c, g) == (1, 2):
                    do_turn_y(0, y1, nxt, 1)
                if not first:
                    if (c, g) == (2, 2):
                        do_turn_y(1, y2, prev, 0)
                    if (c, g) == (3, 1):
                        do_turn_y(1, y2, prev, 1)
                    if (c, g) == (3, 3):
                        do_ffn(prev, 0)
                if not last and (c, g) in AHEAD:
                    qkv(nxt, AHEAD.index((c, g)))
                if last and c > 0 and g % 2 == 1:
                    out_proj(b, c - 1, (g // 2,))
                if not first and (c, g) == (3, 3):
                    do_ffn(prev, 1)

            def run(b, first, last):
                prev, nxt = b + -1, b + 1

                def step(i):
                    if first:
                        qkv(b, C + i)
                    else:
                        out_proj(prev, i // 2, (i % 2,))

                if not first:
                    qkv(b, N_THIRDS - 3)
                    misc_read.append((s_out, added(b + -2, 2)))
                    qkv(b, N_THIRDS - 2)
                if not last:
                    do_turn_a(nxt)
                if not first:
                    qkv(b, N_THIRDS - 1)
                step(0)
                k_sums(b)
                turn_k(b)
                step(1)
                if not last:
                    do_lora(nxt, 0)
                turn_q(b)
                step(2)
                step(3)
                if not last:
                    do_lora(nxt, 1)
                step(4)
                weights(b, 0, 0)
                weights(b, 0, 1)
                step(5)
                for c in range(C):
                    cross(b, c, 0)
                    for half in range(2):
                        for i in range(2):
                            if half == 0:
                                weights(b, c, 2 + i)
                            elif c < C - 1:
                                weights(b, c + 1, i)
                        if c == 0:
                            step(6 + half)
                        between(b, c, 2 * half, first, last)
                        for g in (2 * half, 2 * half + 1):
                            attend(b, c, g)
                        if half == 0:
                            cross(b, c, 1)
                            if c < C - 1:
                                state(b, c)
                        between(b, c, 2 * half + 1, first, last)
                if not last:
                    misc_read.clear()
            iterations(pe, run)

            e = Batch(BATCHES - 1)
            out_proj(e, C - 1)
            do_turn_y(1, y2, e, 0)
            do_ffn(e, 0)
            do_turn_y(1, y2, e, 1)
            do_ffn(e, 1)

        @block.scalar
        def _(act):
            def copy(dst, src):
                return nc.scalar.activation(dst, src, ACT.Copy)

            def v_copy(b, n):
                act.wait_ge(s_vmm, done(b, N_THIRDS, n + 1))
                c, j = third(b, n)
                src = third_ps(n)
                if j < 2:
                    copy(V[:, c, j * THIRD:(j + 1) * THIRD], src).then_inc(s_vev, 1)
                else:
                    copy(V[:, c, 2 * THIRD:HE], src[:, 0:VLAST])
                    nc.scalar.activation(th[:, c, :], src[:, VLAST:THIRD], ACT.Tanh).then_inc(s_vev, 1)

            def features(b):
                th_whole = C if b.reg is None and b.fixed == 0 else N_THIRDS
                act.wait_ge(s_vev, done(b, N_THIRDS, th_whole))
                for f, ready, o in ((fk, s_fk, H), (fq, s_fq, 0)):
                    pairs = f[:, :, :].rearrange("p c (h f) -> p c h f", f=FEAT)
                    nc.scalar.activation(pairs[:, :, :, 0], th[:, :, o:o + H], ACT.Sin, scale=QUARTER_PI,
                                         bias=cst[:, C_HALFPI:C_HALFPI + 1])
                    nc.scalar.activation(pairs[:, :, :, 1], th[:, :, o:o + H], ACT.Sin,
                                         scale=QUARTER_PI).then_inc(ready, 1)

            def hi_of_turned(src, turned, ready, mixed_before):
                act.wait_ge(*turned)
                if mixed_before is not None:
                    act.wait_ge(*mixed_before)
                copy(round_hi[:, 0:src.shape[1]], src).then_inc(ready, 1)

            def k_groups(b):
                act.wait_ge(s_kmix, done(b, 1, 1))
                act.wait_ge(s_gzero, 1)
                for g in range(G):
                    rows = slice(32 * g, 32 * (g + 1))
                    last = copy(k_group[rows, g, :], k_mix[rows, :])
                last.then_inc(s_kgrp, 1)

            def q_groups(b):
                act.wait_ge(s_qmix, done(b, 1, 1))
                for g in range(G):
                    rows = slice(32 * g, 32 * (g + 1))
                    last = copy(q_group[rows, g, :], q_mix[rows, :])
                last.then_inc(s_qgrp, 1)

            def keep(b, first):
                if not first:
                    act.wait_ge(s_h2b, done(b + -1, 2, 2))
                    act.wait_ge(s_y[1], done(b + -1, 2, 2))
                copy(h2[:, :, :], h1[:, b.parity, :, :]).then_inc(s_keep, 1)

            def y_hi(which, hi, b, pair):
                act.wait_ge(s_ytp[which], done(b, 2, pair + 1))
                copy(hi[:, :, 2 * pair * P:2 * (pair + 1) * P], misc.rearrange("p (k t) -> p k t", k=KD))\
                    .then_inc(s_yhi[which], 1)

            def state_hi(b, c):
                act.wait_ge(s_stm, done(b, C - 1, c + 1))
                copy(st_hi[:, :], st_mask[:, :, :].rearrange("p h e -> p (h e)")).then_inc(s_sthi, 1)

            def heads_hi(b, c, half):
                act.wait_ge(s_at, done(b, C * G, c * G + 2 * half + 2))
                i = slice(4 * half, 4 * half + 4)
                copy(at_hi[:, i, c, :], heads_ps[:, i, :]).then_inc(s_athi, 1)

            act.dma_start(cst[:, :], consts).then_inc(s_cst, 16)
            act.wait_ge(s_factors, 16 * FACTORS)
            act.dma_start(raw_qkv, wqkv.rearrange("(k p) n -> p k n", p=P)).then_inc(s_wqkv, 16)
            act.wait_ge(s_cst, 16)
            nc.scalar.activation(rden[:, 0:1], cst[:, 0:1], ACT.Silu)
            act.wait_ge(s_lb2, 1)
            copy(round_hi[:, 0:D], lb2).then_inc(s_lbhi, 1)
            act.wait_ge(s_low, 1)
            copy(low1[0:4, :], misc[0:4, 0:D]).then_inc(s_lowc, 1)
            act.wait_ge(s_low, 2)
            copy(low2[0:50, :], misc[0:50, 0:D]).then_inc(s_lowc, 1)
            act.wait_ge(s_wqkv, 16)
            copy(wqkv_hi[:, :, :], raw_qkv).then_inc(s_whi, 1)
            b0 = Batch(0)
            hi_of_turned(misc[:, 0:P], (s_atp, 1), s_ahi, (s_lball, 1))
            y_hi(0, y1_hi, b0, 0)
            act.wait_ge(s_wdone, 1)
            v_copy(b0, 0)
            y_hi(0, y1_hi, b0, 1)
            for n in range(1, C):
                v_copy(b0, n)

            def run(b, first, last):
                prev, nxt = b + -1, b + 1

                def left(*steps):
                    if first:
                        for i in steps:
                            v_copy(b, C + i)

                if not first:
                    v_copy(b, N_THIRDS - 3)
                    v_copy(b, N_THIRDS - 2)
                if not last:
                    hi_of_turned(misc[:, 0:P], (s_atp, done(nxt, 1, 1)), s_ahi, None)
                if not first:
                    v_copy(b, N_THIRDS - 1)
                features(b)
                left(0)
                hi_of_turned(kt_ps, (s_ktp, done(b, 1, 1)), s_khi, (s_ast, done(nxt if not last else b, 1, 1)))
                left(1)
                hi_of_turned(qt_ps, (s_qtp, done(b, 1, 1)), s_qhi, (s_kmix, done(b, 1, 1)))
                left(2)
                k_groups(b)
                left(3, 4)
                q_groups(b)
                left(5)
                for c in range(C):
                    def ahead(*slots):
                        if not last:
                            for n, place in enumerate(AHEAD):
                                if place[0] == c and place[1] in slots:
                                    v_copy(nxt, n)

                    if c == 0:
                        left(6)
                    heads_hi(b, c, 0)
                    if c < C - 1:
                        state_hi(b, c)
                    else:
                        if not first:
                            y_hi(1, y2_hi, prev, 1)
                        keep(b, first)
                    if c == 0:
                        if not last:
                            y_hi(0, y1_hi, nxt, 0)
                        left(7)
                    ahead(1, 2)
                    if c == 1 and not last:
                        y_hi(0, y1_hi, nxt, 1)
                    if c == 2 and not first:
                        y_hi(1, y2_hi, prev, 0)
                    heads_hi(b, c, 1)
                    ahead(3)
                    if c == 1 and first:
                        act.wait_ge(s_wo, 16)
                        copy(wo_hi[:, :, :], raw_wo).then_inc(s_whi, 1)
                        act.wait_ge(s_wff, 1)
                        copy(wff_hi[:, :, :], raw_ff).then_inc(s_whi, 1)
                if last:
                    y_hi(1, y2_hi, b, 0)
            iterations(act, run)
            y_hi(1, y2_hi, Batch(BATCHES - 1), 1)

        @block.vector
        def _(dve):
            tt = nc.vector.tensor_tensor

            def stack(dst, hi, whole, lo_rows):
                return nc.vector.scalar_tensor_tensor(dst, hi.bitcast(F32), lo_rows, whole, ALU.mult, ALU.add)

            def a_copies(b):
                dve.wait_ge(s_gather[b.parity], done_parity(b, 16 * C, 16 * C))
                nc.vector.tensor_copy(
                    a_rep[:, :].rearrange("p (c n r) -> p c n r", n=COPIES, r=R),
                    emb[:, b.parity, :, D:ROW].unsqueeze(2).to_broadcast([P, C, COPIES, R])).then_inc(s_arep, 1)

            def a_to_stack(b):
                dve.wait_ge(s_ahi, done(b, 1, 1))
                stack(a_stack[:, :], round_hi[:, 0:P], misc[:, 0:P], lo_k).then_inc(s_ast, 1)

            def add_lora(b, pair):
                dve.wait_ge(s_lora, done(b, 2, pair + 1))
                if b.reg is not None or b.fixed >= 2:
                    dve.wait_ge(s_keep, done(b + -2, 1, 1))
                tt(h1[:, b.parity, 2 * pair:2 * pair + 2, :], emb[:, b.parity, 2 * pair:2 * pair + 2, 0:D],
                   misc_pair, ALU.add).then_inc(s_h1, 1)

            def norm_stats(which, x, ready, b, pair):
                dve.wait_ge(*ready)
                tiles = range(2 * pair, 2 * pair + 2)
                for c in tiles:
                    last = nc.vector.bn_stats(ln[which][:, c, :], x[:, c, :])
                last.then_inc(s_stats[which], 1)
                dve.wait_ge(s_cst, 16)
                dve.wait_ge(s_stats[which], done(b, 2, pair + 1))
                for c in tiles:
                    last = nc.vector.bn_aggr(ln_mv[which][:, c, :], ln[which][:, c, :])
                last.then_inc(s_mv[which], 1)

            def norm_apply(which, x, y, b, pair):
                dve.wait_ge(s_rstd[which], done(b, 2, pair + 1))
                for c in range(2 * pair, 2 * pair + 2):
                    last = nc.vector.tensor_scalar(y[:, c, :], x[:, c, :], ln_mv[which][:, c, 0:1],
                                                   ln_rstd[which][:, c:c + 1], ALU.subtract, ALU.mult)
                last.then_inc(s_y[which], 1)

            def y_lo(which, hi, lo, b, pair):
                dve.wait_ge(s_yhi[which], done(b, 2, pair + 1))
                t = slice(2 * pair * P, 2 * (pair + 1) * P)
                tt(lo[:, :, t], misc.rearrange("p (k t) -> p k t", k=KD), hi[:, :, t].bitcast(F32),
                   ALU.subtract).then_inc(s_ylo[which], 1)

            def k_copies(b):
                dve.wait_ge(s_fk, done(b, 1, 1))
                nc.vector.tensor_copy(
                    k_rep[:, :, :].rearrange("p c (g n x) -> p (c g) n x", g=G, n=COPIES),
                    fk[:, :, :].rearrange("p c (g x) -> p (c g) x", g=G).unsqueeze(2)
                    .to_broadcast([P, C * G, COPIES, HG * FEAT])).then_inc(s_krep, 1)

            def q_over_den(b):
                dve.wait_ge(s_fq, done(b, 1, 1))
                dve.wait_ge(s_cumk, done(b, 1, 1))
                flat = lambda x: x[:, :, :].rearrange("p c n -> p (c n)")
                tt(flat(prod), flat(fq), sums_ps, ALU.mult).then_inc(s_prod, 1)
                dve.wait_ge(s_prod, done(b, 1, 1))
                pairs = flat(prod).rearrange("p (n f) -> p n f", f=FEAT)
                nc.vector.scalar_tensor_tensor(den[:, :], pairs[:, :, 0], DEN_EPS, pairs[:, :, 1], ALU.add,
                                               ALU.add).then_inc(s_den, 1)
                dve.wait_ge(s_den, done(b, 1, 1))
                nc.vector.reciprocal(rden[:, :], den[:, :]).then_inc(s_rden, 1)
                dve.wait_ge(s_rden, done(b, 1, 1))
                tt(flat(fqn).rearrange("p (n f) -> p n f", f=FEAT), flat(fq).rearrange("p (n f) -> p n f", f=FEAT),
                   rden[:, :].unsqueeze(2).to_broadcast([P, C * H, FEAT]), ALU.mult).then_inc(s_fqn, 1)
                dve.wait_ge(s_fqn, done(b, 1, 1))
                nc.vector.tensor_copy(
                    q_rep[:, :, :].rearrange("p c (g n x) -> p (c g) n x", g=G, n=COPIES),
                    fqn[:, :, :].rearrange("p c (g x) -> p (c g) x", g=G).unsqueeze(2)
                    .to_broadcast([P, C * G, COPIES, HG * FEAT])).then_inc(s_qrep, 1)

            def k_to_mix(b, first):
                dve.wait_ge(s_khi, done(b, 1, 1))
                if not first:
                    dve.wait_ge(s_kgrp, done(b + -1, 1, 1))
                stack(k_mix[:, :], round_hi[:, :], kt_ps, lo_k).then_inc(s_kmix, 1)

            def q_to_mix(b, first):
                dve.wait_ge(s_qhi, done(b, 1, 1))
                if not first:
                    dve.wait_ge(s_qgrp, done(b + -1, 1, 1))
                stack(q_mix[:, :], round_hi[:, :], qt_ps, lo_q).then_inc(s_qmix, 1)

            def q_heads(b):
                dve.wait_ge(s_qmix, done(b, 1, 1))
                for h in range(HG):
                    last = nc.vector.tensor_scalar(q_head[:, h, :], q_mix[:, :], cst[:, C_HEAD + h:C_HEAD + h + 1],
                                                   None, ALU.mult)
                last.then_inc(s_qhead, 1)

            def add_attention(b, pair):
                dve.wait_ge(s_omm, done(b, 2, pair + 1))
                dve.wait_ge(s_keep, done(b, 1, 1))
                h = h2[:, 2 * pair:2 * pair + 2, :]
                tt(h, h, proj_ps[pair], ALU.add).then_inc(s_h2, 1)

            def mask(b, c, g):
                n = c * G + g
                dve.wait_ge(s_wmm, done(b, C * G, n + 1))
                if c >= 2:
                    dve.wait_ge(s_at, done(b, C * G, n - 2 * G + 1))
                tt(wts[:, c % 2, g * HG:(g + 1) * HG, :], ps[:, 5 + n % 2, :].rearrange("p (h t) -> p h t", t=P),
                   causal.unsqueeze(1).to_broadcast([P, HG, P]), ALU.mult).then_inc(s_wts, 1)

            def mask_state(b, c):
                dve.wait_ge(s_stmm, done(b, C - 1, c + 1))
                tt(st_mask[:, :, :], state_ps.rearrange("p (h e) -> p h e", e=E),
                   cst[:, C_HEAD:C_HEAD + HG].unsqueeze(2).to_broadcast([P, HG, E]), ALU.mult).then_inc(s_stm, 1)

            def state_to_stack(b, c):
                dve.wait_ge(s_sthi, done(b, C - 1, c + 1))
                stack(st[:, :], st_hi[:, :], st_mask[:, :, :].rearrange("p h e -> p (h e)"), lo_k).then_inc(s_st, 1)

            def heads_lo(b, c, half):
                dve.wait_ge(s_athi, done(b, 2 * C, 2 * c + half + 1))
                i = slice(4 * half, 4 * half + 4)
                tt(at_lo[:, i, c, :], heads_ps[:, i, :], at_hi[:, i, c, :].bitcast(F32), ALU.subtract)\
                    .then_inc(s_atlo, 1)

            def add_ffn(b, pair):
                dve.wait_ge(s_ffmm, done(b, 2, pair + 1))
                dve.wait_ge(s_h2b, done(b, 2, pair + 1))
                o = outb[:, b.parity, 2 * pair:2 * pair + 2, :]
                tt(o, o, misc_pair, ALU.add).then_inc(s_out, 1)

            nc.vector.sem_inc(s_out, 2)
            b0 = Batch(0)
            dve.wait_ge(s_lb, 16)
            nc.vector.tensor_scalar(lb2, raw_lb, LORA_SCALE, None, ALU.mult).then_inc(s_lb2, 1)
            dve.wait_ge(s_cst, 16)
            dve.wait_ge(s_lbhi, 1)
            stack(lb_all, round_hi[:, 0:D], lb2, lo_q).then_inc(s_lball, 1)
            dve.wait_ge(s_lball, 1)
            for c in range(C):
                last = nc.vector.tensor_scalar(lb_tiles[:, c, :], lb_all, cst[:, C_TILE + c:C_TILE + c + 1], None,
                                               ALU.mult)
            last.then_inc(s_lbs, 1)
            dve.wait_ge(s_ff, 16)
            dve.wait_ge(s_low, 3)
            tt(raw_ff, raw_ff, misc_pair, ALU.add).then_inc(s_wff, 1)

            def weight_lo(n, lo, whole, hi, slabs):
                dve.wait_ge(s_whi, n)
                return tt(lo[:, slabs, :], whole[:, slabs, :], hi[:, slabs, :].bitcast(F32), ALU.subtract)

            a_copies(b0)
            weight_lo(1, wqkv_lo, raw_qkv, wqkv_hi, slice(0, 1))
            a_to_stack(b0)
            weight_lo(1, wqkv_lo, raw_qkv, wqkv_hi, slice(1, KD)).then_inc(s_wdone, 1)
            add_lora(b0, 0)
            norm_stats(0, h1[:, 0, :, :], (s_h1, 1), b0, 0)
            add_lora(b0, 1)
            norm_apply(0, h1[:, 0, :, :], y1, b0, 0)
            norm_stats(0, h1[:, 0, :, :], (s_h1, 2), b0, 1)
            y_lo(0, y1_hi, y1_lo, b0, 0)
            norm_apply(0, h1[:, 0, :, :], y1, b0, 1)
            y_lo(0, y1_hi, y1_lo, b0, 1)

            def run(b, first, last):
                prev, nxt = b + -1, b + 1
                x1 = h1[:, nxt.parity, :, :]

                def stats(which, pair):
                    if which == 0 and not last:
                        norm_stats(0, x1, (s_h1, done(nxt, 2, pair + 1)), nxt, pair)
                    if which == 1 and not first:
                        norm_stats(1, h2, (s_h2, done(prev, 2, pair + 1)), prev, pair)

                def apply(which, pair):
                    if which == 0 and not last:
                        norm_apply(0, x1, y1, nxt, pair)
                    if which == 1 and not first:
                        norm_apply(1, h2, y2, prev, pair)

                def lo(which, pair):
                    if which == 0 and not last:
                        y_lo(0, y1_hi, y1_lo, nxt, pair)
                    if which == 1 and not first:
                        y_lo(1, y2_hi, y2_lo, prev, pair)

                if not last:
                    a_copies(nxt)
                    a_to_stack(nxt)
                k_copies(b)
                q_over_den(b)
                k_to_mix(b, first)
                if not last:
                    add_lora(nxt, 0)
                q_to_mix(b, first)
                q_heads(b)
                stats(0, 0)
                mask(b, 0, 0)
                mask(b, 0, 1)
                if not last:
                    add_lora(nxt, 1)
                for c in range(C):
                    mask(b, c, 2)
                    mask(b, c, 3)
                    if c < 2:
                        apply(0, c)
                    if c == 2:
                        apply(1, 0)
                    if c < C - 1:
                        mask_state(b, c)
                    heads_lo(b, c, 0)
                    if c < C - 1:
                        state_to_stack(b, c)
                        if c == 0:
                            if not first:
                                add_attention(prev, 0)
                            lo(0, 0)
                        if c == 2 and first:
                            weight_lo(2, wo_lo, raw_wo, wo_hi, slice(0, PAIRS // 2))
                        mask(b, c + 1, 0)
                        mask(b, c + 1, 1)
                        if c == 0:
                            if not first:
                                add_attention(prev, 1)
                        if c == 1:
                            lo(0, 1)
                        if c == 2:
                            stats(1, 1)
                            lo(1, 0)
                    else:
                        lo(1, 1)
                        if first:
                            weight_lo(3, wff_lo, raw_ff, wff_hi, slice(0, KD)).then_inc(s_wdone, 1)
                    if c == 3 and last:
                        add_attention(b, 0)
                        norm_stats(1, h2, (s_h2, done(b, 2, 1)), b, 0)
                    heads_lo(b, c, 1)
                    if c == 0:
                        stats(0, 1)
                    if c == 1:
                        stats(1, 0)
                    if c == 2:
                        apply(1, 1)
                        if first:
                            weight_lo(2, wo_lo, raw_wo, wo_hi, slice(PAIRS // 2, PAIRS)).then_inc(s_wdone, 1)
                    if c == 3 and not first:
                        add_ffn(prev, 0)
                        add_ffn(prev, 1)
                    if c == 3 and last:
                        norm_apply(1, h2, y2, b, 0)
            iterations(dve, run)

            e = Batch(BATCHES - 1)
            add_attention(e, 1)
            norm_stats(1, h2, (s_h2, done(e, 2, 2)), e, 1)
            y_lo(1, y2_hi, y2_lo, e, 0)
            norm_apply(1, h2, y2, e, 1)
            add_ffn(e, 0)
            y_lo(1, y2_hi, y2_lo, e, 1)
            add_ffn(e, 1)


def constants():
    import numpy as np
    a = np.zeros((P, N_CONST), np.float32)
    row = np.arange(P)
    a[:, C_CAUSAL:C_CAUSAL + P] = row[:, None] <= row[None, :]
    a[:, C_ONES:C_ONES + P] = 1
    a[:, C_IDENT:C_IDENT + P] = np.eye(P)
    copy = row // (HG * FEAT) % COPIES
    a[:, C_LO_K] = -1.0 * (copy >= 2)
    a[:, C_LO_Q] = -1.0 * (copy % 2)
    for h in range(HG):
        a[:, C_HEAD + h] = row // FEAT % HG == h
    for c in range(C):
        a[:, C_TILE + c] = row // (COPIES * R) == c
    a[:, C_HALFPI] = np.pi / 2
    a[:, C_EPS] = LN_EPS
    a[:, C_POWER] = -0.5
    return a


def kernel(x, L0_tok_W, L0_tok_lora_A, L0_tok_lora_B, L0_attn_W_Q, L0_attn_W_K, L0_attn_W_V, L0_attn_W_O,
           L0_ffn_W, L0_ffn_b, L0_ffn_lora_down, L0_ffn_lora_up, L0_ffn_down_aux, L0_ffn_up_aux):
    import numpy as np
    import concourse.bacc as bacc
    from concourse.bass_utils import run_bass_kernel_spmd

    layout = {
        "idx": np.asarray(x).reshape(BATCHES * C, P).T,
        "table": np.concatenate([np.asarray(L0_tok_W), np.asarray(L0_tok_lora_A).T], axis=1),
        "wqkv": np.concatenate([np.asarray(L0_attn_W_V).transpose(1, 0, 2).reshape(D, HE),
                                np.asarray(L0_attn_W_Q)[:, :, 0].T, np.asarray(L0_attn_W_K)[:, :, 0].T], axis=1),
        "wo": np.asarray(L0_attn_W_O).transpose(2, 1, 0).reshape(HE, D),
        "wff": np.asarray(L0_ffn_W).T,
        "ld_t": np.asarray(L0_ffn_lora_down).T,
        "lu_t": np.asarray(L0_ffn_lora_up).T,
        "da": np.asarray(L0_ffn_down_aux),
        "ua_t": np.asarray(L0_ffn_up_aux).T,
        "lb_t": np.tile(np.asarray(L0_tok_lora_B).T, (C * COPIES, 1)),
        "bias": np.asarray(L0_ffn_b),
        "consts": constants(),
    }
    nc = bacc.Bacc("TRN2", target_bir_lowering=False, num_devices=1)
    arrays, args = {}, []
    for name, a in layout.items():
        a = np.ascontiguousarray(a)
        arrays[f"in_{name}"] = a
        args.append(nc.dram_tensor(f"in_{name}", a.shape, mybir.dt.from_np(a.dtype), kind="ExternalInput").ap())
    args.append(nc.dram_tensor("out_h", (BATCHES * T, D), F32, kind="ExternalOutput").ap())
    tower(nc, *args)
    r = run_bass_kernel_spmd(nc, [arrays], core_ids=[0])
    return r.results[0]["out_h"].reshape(BATCHES, T, D)
```

```python
from contextlib import ExitStack

import concourse.bass as bass
from concourse import mybir

F32 = mybir.dt.float32
F32R = mybir.dt.float32r
I32 = mybir.dt.int32
ALU = mybir.AluOpType
ACT = mybir.ActivationFunctionType

P = 128
BATCHES = 8
C = 4
T = C * P
D = 256
KD = D // P
H = 16
E = 64
HE = H * E
PAIRS = HE // P
G = 4
HG = H // G
FEAT = 2
R = 8
COPIES = 4
QKV = HE + 2 * H
THIRD = QKV // 3
VLAST = HE - 2 * THIRD
ROW = D + R
LN_EPS = 1e-5
DEN_EPS = 1e-6
LORA_SCALE = 16.0 / 8.0
QUARTER_PI = 3.141592653589793 / 4

FACTORS = 4
N_THIRDS = 3 * C

C_CAUSAL, C_ONES, C_IDENT = 0, P, 2 * P
C_LO_K, C_LO_Q, C_HEAD, C_HALFPI = 3 * P, 3 * P + 1, 3 * P + 2, 3 * P + 2 + HG
C_EPS, C_POWER, C_TILE = C_HALFPI + 1, C_HALFPI + 2, C_HALFPI + 3
N_CONST = C_TILE + C


STEPS = [0, 4, 9, 12, 16, 20, 24, 28, 32]
AHEAD = [(0, 3), (1, 1), (1, 2), (1, 3), (2, 1), (2, 2), (2, 3), (3, 1), (3, 3)]


class Batch:

    def __init__(self, fixed, reg=None):
        self.fixed, self.reg = fixed, reg
        self.parity = fixed % 2

    def __add__(self, n):
        return Batch(self.fixed + n, self.reg)

    def times(self, n, k=0):
        v = self.fixed * n + k
        return v if self.reg is None else self.reg * (2 * n) + v


def third(b, n):
    if b.reg is None and b.fixed == 0:
        return (n, 2) if n < C else ((n - C) // 2, (n - C) % 2)
    return n // 3, n % 3


def done(b, per, k):
    return b.times(per, k)


def done_parity(b, per, k):
    v = (b.fixed // 2) * per + k
    return v if b.reg is None else b.reg * per + v


def tiles(b, part, last_parts=True):
    if last_parts and b.reg is None and b.fixed == BATCHES - 1:
        return (slice(0, 2), slice(2, 3), slice(3, 4))[part]
    return slice(2 * part, 2 * part + 2)


def tower(nc, idx, table, wqkv, wo, wff, ld_t, lu_t, da, ua_t, lb_t, bias, consts, out):
    with ExitStack() as ctx:
        def sb(name, shape, dt=F32):
            return ctx.enter_context(nc.sbuf_tensor(name, shape, dt))

        def sem(name):
            return ctx.enter_context(nc.semaphore(name))

        cst = sb("cst", [P, N_CONST])
        causal, ones, ident = (cst[:, o:o + P] for o in (C_CAUSAL, C_ONES, C_IDENT))
        lo_k, lo_q = cst[:, C_LO_K:C_LO_K + 1], cst[:, C_LO_Q:C_LO_Q + 1]
        idx_sb = sb("idx_sb", [P, BATCHES * C], I32)
        idx_cur = sb("idx_cur", [P, 2, C], I32)
        idx_seen = sb("idx_seen", [P, C], I32)
        wqkv_hi, wqkv_lo = (sb(f"wqkv_{n}", [P, KD, QKV], F32R) for n in ("hi", "lo"))
        wo_hi, wo_lo = (sb(f"wo_{n}", [P, PAIRS, D], F32R) for n in ("hi", "lo"))
        wff_hi, wff_lo = (sb(f"wff_{n}", [P, KD, D], F32R) for n in ("hi", "lo"))
        lb_tiles = sb("lb_tiles", [P, C, D], F32R)
        bias_sb = sb("bias_sb", [P, D])
        emb = sb("emb", [P, 2, C, ROW])
        a_rep = sb("a_rep", [P, C * COPIES * R])
        a_stack = sb("a_stack", [P, P], F32R)
        h1 = sb("h1", [P, 2, C, D])
        h2 = sb("h2", [P, C, D])
        y1, y2 = sb("y1", [P, C, D]), sb("y2", [P, C, D])
        y1_hi, y1_lo = (sb(f"y1_{n}", [P, KD, T], F32R) for n in ("hi", "lo"))
        y2_hi, y2_lo = (sb(f"y2_{n}", [P, KD, T], F32R) for n in ("hi", "lo"))
        ln = [sb(f"ln{i}", [P, C, 6]) for i in (1, 2)]
        ln_mv = [sb(f"ln_mv{i}", [P, C, 2]) for i in (1, 2)]
        ln_ve = [sb(f"ln_ve{i}", [P, C]) for i in (1, 2)]
        ln_rstd = [sb(f"ln_rstd{i}", [P, C]) for i in (1, 2)]
        V = sb("V", [P, C, HE])
        th = sb("th", [P, C, 2 * H])
        fq, fk = sb("fq", [P, C, H * FEAT]), sb("fk", [P, C, H * FEAT])
        prod = sb("prod", [P, C, H * FEAT])
        den, rden = sb("den", [P, C * H]), sb("rden", [P, C * H])
        fqn = sb("fqn", [P, C, H * FEAT])
        k_rep, q_rep = sb("k_rep", [P, C, P]), sb("q_rep", [P, C, P])
        round_hi = sb("round_hi", [P, T], F32R)
        k_mix, q_mix = sb("k_mix", [P, T]), sb("q_mix", [P, T])
        k_group = sb("k_group", [P, G, T], F32R)
        q_group = sb("q_group", [P, G, T], F32R)
        q_head = sb("q_head", [P, HG, T], F32R)
        wts = sb("wts", [P, 2, H, P])
        st_mask = sb("st_mask", [P, HG, E])
        st_hi = sb("st_hi", [P, HG * E], F32R)
        st = sb("st", [P, HG * E], F32R)
        at_hi, at_lo = (sb(f"at_{n}", [P, PAIRS, C, P], F32R) for n in ("hi", "lo"))
        outb = sb("outb", [P, 2, C, D])
        raw_qkv = V[:, :, :].rearrange("p c n -> p (c n)")[:, 0:KD * QKV].rearrange("p (k n) -> p k n", k=KD)
        raw_wo = outb[:, :, :, :].rearrange("p a c n -> p (a c) n")
        raw_ff = sb("raw_ff", [P, KD, D])[:, :, :]
        raw_da, raw_ua, raw_ld, raw_lu = (h2[:, i, :] for i in range(4))
        raw_lb, low1, low2, lb2 = (y2[:, i, :] for i in range(4))
        lb_all = y1[:, 0, :]

        ps = ctx.enter_context(nc.psum_tensor("ps", [P, 8, 512], F32))
        heads_ps = ps[:, 0:2, :].rearrange("p a (b t) -> p (a b) t", t=P)
        proj_ps = [ps[:, 4 - i, :].rearrange("p (c n) -> p c n", n=D) for i in range(2)]

        def third_ps(n):
            return ps[:, 3 + (1 + n) % 2, 0:THIRD]
        state_ps = ps[:, 2, 0:HG * E]
        sums_ps = ps[:, 2, HG * E:HG * E + C * H * FEAT]
        qt_ps, kt_ps = ps[:, 5, :], ps[:, 6, :]
        low_ps = ps[:, 6, :]
        low_pair = low_ps.rearrange("p (k n) -> p k n", n=D)
        misc = ps[:, 7, :]
        misc_pair = misc.rearrange("p (c n) -> p c n", n=D)

        s_cst, s_idx, s_wqkv, s_wo, s_lb, s_factors, s_ff, s_bias = (
            sem(n) for n in ("cst_loaded", "idx_loaded", "wqkv_loaded", "wo_loaded", "lora_b_loaded",
                             "low_rank_loaded", "wff_loaded", "bias_loaded"))
        s_gzero, s_low, s_whi, s_wdone, s_lb2, s_lbhi = (
            sem(n) for n in ("group_zeros_ready", "low_rank_mm", "w_hi_ready", "w_ready", "lb2_ready", "lb_hi_ready"))
        s_lowc, s_wff, s_lball, s_lbs = (
            sem(n) for n in ("low_rank_copied", "wff_whole", "lb_stack_ready", "lb_tiles_ready"))
        s_idxc = sem("idx_copied")
        s_gather = [sem(f"gathered{i}") for i in range(2)]
        s_arep, s_atp, s_ahi, s_ast, s_lora, s_h1 = (
            sem(n) for n in ("a_rep_ready", "a_turned", "a_hi_ready", "a_stack_ready", "lora_mm", "h1_ready"))
        s_stats = [sem(f"ln{i}_stats") for i in (1, 2)]
        s_mv = [sem(f"ln{i}_mean_var") for i in (1, 2)]
        s_ve = [sem(f"ln{i}_var_eps") for i in (1, 2)]
        s_rstd = [sem(f"ln{i}_rstd") for i in (1, 2)]
        s_y = [sem(f"y{i}_ready") for i in (1, 2)]
        s_ytp = [sem(f"y{i}_turned") for i in (1, 2)]
        s_yhi = [sem(f"y{i}_hi_ready") for i in (1, 2)]
        s_ylo = [sem(f"y{i}_lo_ready") for i in (1, 2)]
        s_vmm, s_vev, s_fk, s_fq, s_cumk = (
            sem(n) for n in ("qkv_mm", "qkv_copied", "k_features", "q_features", "k_sums_mm"))
        s_krep, s_prod, s_den, s_rden, s_fqn, s_qrep = (
            sem(n) for n in ("k_rep_ready", "den_products", "den_ready", "rden_ready", "fqn_ready", "q_rep_ready"))
        s_ktp, s_khi, s_kmix, s_kgrp = (sem(n) for n in ("k_turned", "k_hi_ready", "k_mix_ready", "k_group_ready"))
        s_qtp, s_qhi, s_qmix, s_qhead, s_qgrp = (
            sem(n) for n in ("q_turned", "q_hi_ready", "q_mix_ready", "q_head_ready", "q_group_ready"))
        s_wmm, s_wts, s_at = sem("weights_mm"), sem("weights_masked"), sem("attention_mm")
        s_stmm, s_stm, s_sthi, s_st = (
            sem(n) for n in ("state_mm", "state_masked", "state_hi_ready", "state_ready"))
        s_athi, s_atlo = sem("at_hi_ready"), sem("at_lo_ready")
        s_keep, s_cross = sem("h1_kept"), sem("cross_mm")
        s_omm, s_h2, s_h2b, s_ffmm, s_out = (
            sem(n) for n in ("proj_mm", "h2_ready", "h2_bias_added", "ffn_mm", "out_ready"))
        s_stored = [sem(f"stored{i}") for i in range(2)]

        def iterations(eng, run):
            run(Batch(0), True, False)
            with eng.Fori(0, (BATCHES - 2) // 2) as i:
                run(Batch(1, i), False, False)
                run(Batch(2, i), False, False)
            run(Batch(BATCHES - 1), False, True)

        def is_end(b):
            return b.reg is None and b.fixed == BATCHES - 1

        def projected(b, c):
            if is_end(b) and c.start == C - 1:
                return proj_ps[0][:, 0:1, :]
            return proj_ps[c.start // 2][:, c.start % 2:c.start % 2 + c.stop - c.start, :]

        def turned(which, b):
            return ps[:, 5, :] if which == 1 and is_end(b) else misc

        def turned_part(which, b, c):
            return turned(which, b).rearrange("p (k t) -> p k t", k=KD)[:, :, 0:(c.stop - c.start) * P]

        def fed(b, part):
            bank = (6, 7, 3)[part] if is_end(b) else 7
            return ps[:, bank, :].rearrange("p (c n) -> p c n", n=D)

        def added(b, pairs):
            return done(b, 2, pairs + 2)

        block = ctx.enter_context(nc.Block())

        @block.sync
        def _(sp):
            for i in range(2):
                sp.sem_inc(s_stored[i], 16)
            sp.dma_start(idx_sb[:, :], idx).then_inc(s_idx, 16)
            for dst, src in ((raw_ld, ld_t), (raw_da, da), (raw_lu, lu_t), (raw_ua, ua_t)):
                sp.dma_start(dst[0:src.shape[0], 0:src.shape[1]], src).then_inc(s_factors, 16)
            sp.dma_start(raw_lb, lb_t).then_inc(s_lb, 16)
            sp.wait_ge(s_gather[0], 16 * C)
            sp.dma_start(raw_ff, wff.rearrange("(k p) n -> p k n", p=P)).then_inc(s_ff, 16)
            sp.dma_start(bias_sb[:, :], bias.partition_broadcast(P)).then_inc(s_bias, 16)
            sp.dma_start(raw_wo, wo.rearrange("(k p) n -> p k n", p=P)).then_inc(s_wo, 16)

            def store(b):
                sp.wait_ge(s_out, added(b, 2))
                rows = out[bass.ds(b.times(T), T), :].rearrange("(c p) n -> p c n", p=P)
                sp.dma_start(rows, outb[:, b.parity, :, :]).then_inc(s_stored[b.parity], 16)

            def run(b, first, last):
                if not first:
                    store(b + -1)
            iterations(sp, run)
            e = Batch(BATCHES - 1)
            for part in range(3):
                sp.wait_ge(s_out, added(e, part + 1))
                c = tiles(e, part)
                rows = out[e.fixed * T + c.start * P:e.fixed * T + c.stop * P, :].rearrange("(c p) n -> p c n", p=P)
                sp.dma_start(rows, outb[:, e.parity, c, :]).then_inc(s_stored[e.parity], 16)
            for i in range(2):
                sp.wait_ge(s_stored[i], 16 * (BATCHES // 2 + 1 + 2 * i))

        @block.gpsimd
        def _(pool):
            def gather(b, fresh=False):
                if not fresh:
                    pool.wait_ge(s_h1, done(b + -2, 2, 2))
                nc.gpsimd.tensor_copy(idx_cur[:, b.parity, :], idx_sb[:, bass.ds(b.times(C), C)]).then_inc(s_idxc, 1)
                pool.wait_ge(s_idxc, done(b, 1, 1))
                nc.gpsimd.tensor_tensor(idx_seen[:, :], idx_cur[:, b.parity, :], idx_cur[:, b.parity, :], ALU.add)
                for c in range(C):
                    pool.indirect_dma_start(
                        out=emb[:, b.parity, c, :], out_offset=None, in_=table,
                        in_offset=bass.IndirectOffsetOnAxis(ap=idx_cur[:, b.parity, c:c + 1], axis=0),
                    ).then_inc(s_gather[b.parity], 16)

            def add_bias(b, pair):
                if b.reg is None and b.fixed == 0:
                    pool.wait_ge(s_bias, 16)
                pool.wait_ge(s_h2, done(b, 2, pair + 1))
                if pair == 0:
                    pool.wait_ge(s_stored[b.parity], done_parity(b, 16, 16))
                c = tiles(b, pair)
                nc.gpsimd.tensor_tensor(outb[:, b.parity, c, :], h2[:, c, :],
                                        bias_sb[:, :].unsqueeze(1).to_broadcast([P, c.stop - c.start, D]),
                                        ALU.add).then_inc(s_h2b, 1)

            def norm_rstd(which, b, pair):
                pool.wait_ge(s_mv[which], done(b, 2, pair + 1))
                c = tiles(b, pair, which == 1)
                cols = [cst[:, i:i + 1].to_broadcast([P, c.stop - c.start]) for i in (C_EPS, C_POWER)]
                nc.gpsimd.tensor_tensor(ln_ve[which][:, c], ln_mv[which][:, c, 1], cols[0],
                                        ALU.add).then_inc(s_ve[which], 1)
                pool.wait_ge(s_ve[which], done(b, 2, pair + 1))
                nc.gpsimd.tensor_tensor(ln_rstd[which][:, c], ln_ve[which][:, c], cols[1],
                                        ALU.pow).then_inc(s_rstd[which], 1)

            pool.wait_ge(s_idx, 16)
            b0 = Batch(0)
            gather(b0, fresh=True)
            for x in (k_group, q_group):
                last = nc.gpsimd.memset(x[:, :, :].bitcast(F32), 0.0)
            last.then_inc(s_gzero, 1)
            gather(Batch(1), fresh=True)
            pool.wait_ge(s_cst, 16)
            norm_rstd(0, b0, 0)
            norm_rstd(0, b0, 1)

            def run(b):
                fixed = b.reg is None
                if not (fixed and b.fixed == BATCHES - 1):
                    norm_rstd(0, b + 1, 0)
                    norm_rstd(0, b + 1, 1)
                if not (fixed and b.fixed >= BATCHES - 2):
                    gather(b + 2)
                if not (fixed and b.fixed == 0):
                    norm_rstd(1, b + -1, 0)
                    norm_rstd(1, b + -1, 1)
                    add_bias(b + -1, 0)
                    add_bias(b + -1, 1)
            for n in range(2):
                run(Batch(n))
            with pool.Fori(0, (BATCHES - 4) // 2) as i:
                run(Batch(2, i))
                run(Batch(3, i))
            for n in range(BATCHES - 2, BATCHES):
                run(Batch(n))
            e = Batch(BATCHES - 1)
            for part in range(3):
                norm_rstd(1, e, part)
                add_bias(e, part)

        @block.tensor
        def _(pe):
            def mm(*args, **kw):
                return nc.tensor.matmul(*args, skip_group_check=True, **kw)

            def split_mm(dst, lhs, rhs, slabs):
                n = 0
                for k in range(slabs):
                    for x, w in ((0, 0), (1, 0), (0, 1)):
                        last = mm(dst, lhs(x, k), rhs(w, k), start=(n == 0), stop=(n == 3 * slabs - 1))
                        n += 1
                return last

            def low_rank():
                pe.wait_ge(s_factors, 16 * FACTORS)
                mm(low_ps[0:4, 0:D], raw_ld[0:100, 0:4], raw_da[0:100, :], start=True, stop=True).then_inc(s_low, 1)
                pe.wait_ge(s_lowc, 1)
                mm(low_ps[0:50, 0:D], raw_lu[0:4, 0:50], low1[0:4, :], start=True, stop=True).then_inc(s_low, 1)
                pe.wait_ge(s_lowc, 2)
                for k in range(KD):
                    last = mm(low_pair[:, k, :], low2[0:50, k * P:(k + 1) * P], raw_ua[0:50, :],
                              start=(k == 0), stop=True)
                last.then_inc(s_low, 1)

            def turn(dst, src):
                for c in range(C):
                    last = nc.tensor.transpose(dst[:, c * P:(c + 1) * P], src(c), ident)
                return last

            def turn_a(b):
                pe.wait_ge(s_arep, done(b, 1, 1))
                nc.tensor.transpose(misc[:, 0:P], a_rep[:, :], ident).then_inc(s_atp, 1)

            def lora(b, pair):
                pe.wait_ge(s_ast, done(b, 1, 1))
                for i in range(2):
                    last = mm(misc_pair[:, i, :], a_stack[:, :], lb_tiles[:, 2 * pair + i, :], start=(i == 0),
                              stop=True)
                last.then_inc(s_lora, 1)

            def turn_y(which, y, b, pair):
                pe.wait_ge(s_y[which], done(b, 2, pair + 1))
                c = tiles(b, pair, which == 1)
                for i in range(c.stop - c.start):
                    for k in range(KD):
                        j = k * 2 + i
                        last = nc.tensor.transpose(turned(which, b)[:, j * P:(j + 1) * P],
                                                   y[:, c.start + i, k * P:(k + 1) * P], ident)
                last.then_inc(s_ytp[which], 1)

            def qkv(b, n):
                parts, w = (y1_hi, y1_lo), (wqkv_hi, wqkv_lo)
                c, j = third(b, n)
                if n == 0 or (c, third(b, n - 1)[0]) == (2, 1):
                    pe.wait_ge(s_ylo[0], done(b, 2, c // 2 + 1))
                if n >= 2:
                    pe.wait_ge(s_vev, done(b, N_THIRDS, n - 1))
                elif b.reg is None and b.fixed == 1:
                    pe.wait_ge(s_vev, done(b + -1, N_THIRDS, N_THIRDS - 1 + n))
                elif b.reg is not None or b.fixed > 0:
                    pe.wait_ge(s_h2, done(b + -2, 2, n + 1))
                split_mm(third_ps(n), lambda x, k: parts[x][:, k, c * P:(c + 1) * P],
                         lambda x, k: w[x][:, k, j * THIRD:(j + 1) * THIRD], KD).then_inc(s_vmm, 1)

            def out_proj(b, first_slab, end_slab):
                if b.reg is None and b.fixed == 0 and first_slab == 0:
                    pe.wait_ge(s_wdone, 3)
                parts, w = (at_hi, at_lo), (wo_hi, wo_lo)
                for slab in range(first_slab, end_slab):
                    c, k = slab // PAIRS, slab % PAIRS
                    dst = projected(b, slice(c, c + 1))[:, 0, :]
                    if k % (PAIRS // 2) == 0 or slab == first_slab:
                        pe.wait_ge(s_atlo, done(b, 2 * C, slab // (PAIRS // 2) + 1))
                    if c % 2 == 0 and k == 0:
                        if b.reg is not None or b.fixed < BATCHES - 1:
                            pe.wait_ge(s_vev, done(b + 1, N_THIRDS, N_THIRDS - 1 + c // 2))
                        else:
                            pe.wait_ge(s_h2, done(b + -1, 2, c // 2 + 1))
                    if c == C - 1 and k == 0 and is_end(b):
                        pe.wait_ge(s_h2, done(b, 2, 1))
                    for x, v in ((0, 0), (1, 0), (0, 1)):
                        last = mm(dst, parts[x][:, k, c, :], w[v][:, k, :], start=(k == 0 and x + v == 0),
                                  stop=(k == PAIRS - 1 and v == 1))
                    if k == PAIRS - 1 and (c % 2 == 1 or (c == 2 and is_end(b))):
                        last.then_inc(s_omm, 1)

            def k_sums(b):
                pe.wait_ge(s_fk, done(b, 1, 1))
                mm(sums_ps, causal, fk[:, :, :].rearrange("p c n -> p (c n)"), start=True, stop=False)
                n = H * FEAT
                for c in range(C - 1):
                    later = C - 1 - c
                    last = mm(sums_ps[:, (c + 1) * n:C * n].rearrange("p (c n) -> p c n", n=n), ones,
                              fk[:, c, :].unsqueeze(1).to_broadcast([P, later, n]), start=False, stop=(c == C - 2))
                last.then_inc(s_cumk, 1)

            def turn_k(b):
                pe.wait_ge(s_krep, done(b, 1, 1))
                turn(kt_ps, lambda c: k_rep[:, c, :]).then_inc(s_ktp, 1)

            def turn_q(b):
                pe.wait_ge(s_qrep, done(b, 1, 1))
                turn(qt_ps, lambda c: q_rep[:, c, :]).then_inc(s_qtp, 1)

            def weights(b, c, g):
                n = c * G + g
                if n == 0:
                    pe.wait_ge(s_kgrp, done(b, 1, 1))
                    pe.wait_ge(s_qhead, done(b, 1, 1))
                if n >= 2:
                    pe.wait_ge(s_wts, done(b, C * G, n - 1))
                mm(ps[:, 5 + n % 2, :].rearrange("p (h t) -> p h t", t=P), k_group[:, g, c * P:(c + 1) * P],
                   q_head[:, :, c * P:(c + 1) * P], start=True, stop=True).then_inc(s_wmm, 1)

            def cross(b, c, half):
                if c > 0:
                    pe.wait_ge(s_atlo, done(b, 2 * C, 2 * c - 1 + half))
                    if half == 0:
                        pe.wait_ge(s_st, done(b, C - 1, c))
                    if (c, half) == (1, 0):
                        pe.wait_ge(s_qgrp, done(b, 1, 1))
                    for i in range(2):
                        last = mm(heads_ps[:, 4 * half + i:4 * half + 4:2, :], st[:, i * P:(i + 1) * P],
                                  q_group[:, 2 * half:2 * half + 2, c * P:(c + 1) * P], start=(i == 0), stop=False)
                    if half == 1:
                        last.then_inc(s_cross, 1)
                elif b.reg is not None or b.fixed > 0:
                    pe.wait_ge(s_atlo, done(b + -1, 2 * C, 2 * C - 1 + half))

            def state(b, c):
                if c > 0:
                    pe.wait_ge(s_stm, done(b, C - 1, c))
                for g in range(G):
                    last = mm(state_ps[32 * g:32 * (g + 1), :], k_rep[:, c, 32 * g:32 * (g + 1)],
                              V[:, c, g * HG * E:(g + 1) * HG * E], start=(c == 0), stop=True,
                              tile_position=(0, 32 * g))
                last.then_inc(s_stmm, 1)

            def attend(b, c, g):
                pe.wait_ge(s_wts, done(b, C * G, c * G + g + 1))
                if b.reg is None and b.fixed == 0 and g == 0:
                    pe.wait_ge(s_vev, C + 2 * (c + 1))
                for h in range(g * HG, (g + 1) * HG):
                    half = slice(64 * (h % 2), 64 * (h % 2) + 64)
                    opens = c == 0 and h % 8 < 2
                    last = mm(heads_ps[half, h // 2, :], V[:, c, h * E:(h + 1) * E], wts[:, c % 2, h, :],
                              start=opens, stop=(h % 8 >= 6))
                last.then_inc(s_at, 1)

            def ffn(b, pair):
                parts, w = (y2_hi, y2_lo), (wff_hi, wff_lo)
                pe.wait_ge(s_ylo[1], done(b, 2, pair + 1))
                tiles_of = tiles(b, pair)
                for c in range(tiles_of.start, tiles_of.stop):
                    last = split_mm(fed(b, pair)[:, c - tiles_of.start, :],
                                    lambda x, k: parts[x][:, k, c * P:(c + 1) * P], lambda x, k: w[x][:, k, :], KD)
                last.then_inc(s_ffmm, 1)

            misc_read = []

            def with_misc(step, *args, until):
                if misc_read:
                    pe.wait_ge(*misc_read.pop())
                step(*args)
                misc_read.append(until)

            def do_turn_a(b):
                with_misc(turn_a, b, until=(s_ast, done(b, 1, 1)))

            def do_lora(b, pair):
                with_misc(lora, b, pair, until=(s_h1, done(b, 2, pair + 1)))

            def do_turn_y(which, y, b, pair):
                with_misc(turn_y, which, y, b, pair, until=(s_ylo[which], done(b, 2, pair + 1)))

            def do_ffn(b, pair):
                with_misc(ffn, b, pair, until=(s_out, added(b, pair + 1)))

            low_rank()
            pe.wait_ge(s_cst, 16)
            b0 = Batch(0)
            do_turn_a(b0)
            pe.wait_ge(s_lbs, 1)
            for pair in range(2):
                do_lora(b0, pair)
            do_turn_y(0, y1, b0, 0)
            pe.wait_ge(s_wdone, 1)
            qkv(b0, 0)
            do_turn_y(0, y1, b0, 1)
            for n in range(1, C):
                qkv(b0, n)

            def between(b, c, g, first, last):
                prev, nxt = b + -1, b + 1
                if not last and (c, g) == (0, 1):
                    do_turn_y(0, y1, nxt, 0)
                if not first:
                    if (c, g) == (2, 2):
                        do_turn_y(1, y2, prev, 0)
                    if (c, g) == (3, 1):
                        do_turn_y(1, y2, prev, 1)
                    if (c, g) == (3, 3):
                        do_ffn(prev, 0)
                if not last and (c, g) in AHEAD:
                    qkv(nxt, AHEAD.index((c, g)))
                if not last and (c, g) == (1, 2):
                    do_turn_y(0, y1, nxt, 1)
                if last and c > 0 and g % 2 == 1:
                    half = 2 * (c - 1) + g // 2
                    out_proj(b, half * PAIRS // 2, (half + 1) * PAIRS // 2)
                if not first and (c, g) == (3, 3):
                    do_ffn(prev, 1)

            def run(b, first, last):
                prev, nxt = b + -1, b + 1

                def step(i):
                    if first:
                        qkv(b, C + i)
                    else:
                        out_proj(prev, STEPS[i], STEPS[i + 1])

                if not first:
                    qkv(b, N_THIRDS - 3)
                    misc_read.append((s_out, added(b + -2, 2)))
                    qkv(b, N_THIRDS - 2)
                if not last:
                    do_turn_a(nxt)
                if not first:
                    qkv(b, N_THIRDS - 1)
                step(0)
                k_sums(b)
                turn_k(b)
                step(1)
                if not last:
                    do_lora(nxt, 0)
                turn_q(b)
                step(2)
                step(3)
                if not last:
                    do_lora(nxt, 1)
                step(4)
                weights(b, 0, 0)
                weights(b, 0, 1)
                step(5)
                for c in range(C):
                    cross(b, c, 0)
                    for half in range(2):
                        for i in range(2):
                            if half == 0:
                                weights(b, c, 2 + i)
                            elif c < C - 1:
                                weights(b, c + 1, i)
                        if c == 0:
                            step(6 + half)
                        between(b, c, 2 * half, first, last)
                        for g in (2 * half, 2 * half + 1):
                            attend(b, c, g)
                        if half == 0:
                            if c < C - 1:
                                state(b, c)
                            cross(b, c, 1)
                        between(b, c, 2 * half + 1, first, last)
                if not last:
                    misc_read.clear()
            iterations(pe, run)

            e = Batch(BATCHES - 1)
            turn_y(1, y2, e, 0)
            out_proj(e, (C - 1) * PAIRS, C * PAIRS)
            ffn(e, 0)
            turn_y(1, y2, e, 1)
            pe.wait_ge(*misc_read.pop())
            ffn(e, 1)
            turn_y(1, y2, e, 2)
            ffn(e, 2)

        @block.scalar
        def _(act):
            def copy(dst, src):
                return nc.scalar.activation(dst, src, ACT.Copy)

            def v_copy(b, n):
                act.wait_ge(s_vmm, done(b, N_THIRDS, n + 1))
                c, j = third(b, n)
                src = third_ps(n)
                if j < 2:
                    copy(V[:, c, j * THIRD:(j + 1) * THIRD], src).then_inc(s_vev, 1)
                else:
                    copy(V[:, c, 2 * THIRD:HE], src[:, 0:VLAST])
                    nc.scalar.activation(th[:, c, :], src[:, VLAST:THIRD], ACT.Tanh).then_inc(s_vev, 1)

            def features(b):
                th_whole = C if b.reg is None and b.fixed == 0 else N_THIRDS
                act.wait_ge(s_vev, done(b, N_THIRDS, th_whole))
                for f, ready, o in ((fk, s_fk, H), (fq, s_fq, 0)):
                    pairs = f[:, :, :].rearrange("p c (h f) -> p c h f", f=FEAT)
                    nc.scalar.activation(pairs[:, :, :, 0], th[:, :, o:o + H], ACT.Sin, scale=QUARTER_PI,
                                         bias=cst[:, C_HALFPI:C_HALFPI + 1])
                    nc.scalar.activation(pairs[:, :, :, 1], th[:, :, o:o + H], ACT.Sin,
                                         scale=QUARTER_PI).then_inc(ready, 1)

            def hi_of_turned(src, turned, ready, mixed_before):
                act.wait_ge(*turned)
                if mixed_before is not None:
                    act.wait_ge(*mixed_before)
                copy(round_hi[:, 0:src.shape[1]], src).then_inc(ready, 1)

            def k_groups(b):
                act.wait_ge(s_kmix, done(b, 1, 1))
                act.wait_ge(s_gzero, 1)
                for g in range(G):
                    rows = slice(32 * g, 32 * (g + 1))
                    last = copy(k_group[rows, g, :], k_mix[rows, :])
                last.then_inc(s_kgrp, 1)

            def q_groups(b):
                act.wait_ge(s_qmix, done(b, 1, 1))
                for g in range(G):
                    rows = slice(32 * g, 32 * (g + 1))
                    last = copy(q_group[rows, g, :], q_mix[rows, :])
                last.then_inc(s_qgrp, 1)

            def keep(b, first):
                if not first:
                    act.wait_ge(s_h2b, done(b + -1, 2, 2))
                    act.wait_ge(s_y[1], done(b + -1, 2, 2))
                copy(h2[:, :, :], h1[:, b.parity, :, :]).then_inc(s_keep, 1)

            def y_hi(which, hi, b, pair):
                act.wait_ge(s_ytp[which], done(b, 2, pair + 1))
                c = tiles(b, pair, which == 1)
                copy(hi[:, :, c.start * P:c.stop * P], turned_part(which, b, c)).then_inc(s_yhi[which], 1)

            def state_hi(b, c):
                act.wait_ge(s_stm, done(b, C - 1, c + 1))
                copy(st_hi[:, :], st_mask[:, :, :].rearrange("p h e -> p (h e)")).then_inc(s_sthi, 1)

            def heads_hi(b, c, half):
                act.wait_ge(s_at, done(b, C * G, c * G + 2 * half + 2))
                i = slice(4 * half, 4 * half + 4)
                copy(at_hi[:, i, c, :], heads_ps[:, i, :]).then_inc(s_athi, 1)

            act.dma_start(cst[:, :], consts).then_inc(s_cst, 16)
            act.wait_ge(s_factors, 16 * FACTORS)
            act.dma_start(raw_qkv, wqkv.rearrange("(k p) n -> p k n", p=P)).then_inc(s_wqkv, 16)
            act.wait_ge(s_cst, 16)
            nc.scalar.activation(rden[:, 0:1], cst[:, 0:1], ACT.Silu)
            act.wait_ge(s_lb2, 1)
            copy(round_hi[:, 0:D], lb2).then_inc(s_lbhi, 1)
            act.wait_ge(s_low, 1)
            copy(low1[0:4, :], low_ps[0:4, 0:D]).then_inc(s_lowc, 1)
            act.wait_ge(s_low, 2)
            copy(low2[0:50, :], low_ps[0:50, 0:D]).then_inc(s_lowc, 1)
            act.wait_ge(s_wqkv, 16)
            copy(wqkv_hi[:, 0, :], raw_qkv[:, 0, :]).then_inc(s_whi, 1)
            b0 = Batch(0)
            hi_of_turned(misc[:, 0:P], (s_atp, 1), s_ahi, (s_lball, 1))
            copy(wqkv_hi[:, 1, :], raw_qkv[:, 1, :]).then_inc(s_whi, 1)
            y_hi(0, y1_hi, b0, 0)
            act.wait_ge(s_wdone, 1)
            v_copy(b0, 0)
            y_hi(0, y1_hi, b0, 1)
            for n in range(1, C):
                v_copy(b0, n)

            def run(b, first, last):
                prev, nxt = b + -1, b + 1

                def left(*steps):
                    if first:
                        for i in steps:
                            v_copy(b, C + i)

                if not first:
                    v_copy(b, N_THIRDS - 3)
                    v_copy(b, N_THIRDS - 2)
                if not last:
                    hi_of_turned(misc[:, 0:P], (s_atp, done(nxt, 1, 1)), s_ahi, None)
                if not first:
                    v_copy(b, N_THIRDS - 1)
                features(b)
                left(0)
                hi_of_turned(kt_ps, (s_ktp, done(b, 1, 1)), s_khi, (s_ast, done(nxt if not last else b, 1, 1)))
                left(1)
                hi_of_turned(qt_ps, (s_qtp, done(b, 1, 1)), s_qhi, (s_kmix, done(b, 1, 1)))
                left(2)
                k_groups(b)
                left(3, 4)
                q_groups(b)
                left(5)
                for c in range(C):
                    def ahead(*slots):
                        if not last:
                            for n, place in enumerate(AHEAD):
                                if place[0] == c and place[1] in slots:
                                    v_copy(nxt, n)

                    if c == 0:
                        left(6)
                    heads_hi(b, c, 0)
                    if c < C - 1:
                        state_hi(b, c)
                    else:
                        if not first:
                            y_hi(1, y2_hi, prev, 1)
                        keep(b, first)
                    if c == 0:
                        if not last:
                            y_hi(0, y1_hi, nxt, 0)
                        left(7)
                    ahead(1, 2)
                    if c == 1 and not last:
                        y_hi(0, y1_hi, nxt, 1)
                    if c == 2 and not first:
                        y_hi(1, y2_hi, prev, 0)
                    heads_hi(b, c, 1)
                    ahead(3)
                    if c == 1 and first:
                        act.wait_ge(s_wo, 16)
                        copy(wo_hi[:, :, :], raw_wo).then_inc(s_whi, 1)
                        act.wait_ge(s_wff, 1)
                        copy(wff_hi[:, :, :], raw_ff).then_inc(s_whi, 1)
            iterations(act, run)
            for part in range(3):
                y_hi(1, y2_hi, Batch(BATCHES - 1), part)

        @block.vector
        def _(dve):
            tt = nc.vector.tensor_tensor

            def stack(dst, hi, whole, lo_rows):
                return nc.vector.scalar_tensor_tensor(dst, hi.bitcast(F32), lo_rows, whole, ALU.mult, ALU.add)

            def a_copies(b):
                dve.wait_ge(s_gather[b.parity], done_parity(b, 16 * C, 16 * C))
                nc.vector.tensor_copy(
                    a_rep[:, :].rearrange("p (c n r) -> p c n r", n=COPIES, r=R),
                    emb[:, b.parity, :, D:ROW].unsqueeze(2).to_broadcast([P, C, COPIES, R])).then_inc(s_arep, 1)

            def a_to_stack(b):
                dve.wait_ge(s_ahi, done(b, 1, 1))
                stack(a_stack[:, :], round_hi[:, 0:P], misc[:, 0:P], lo_k).then_inc(s_ast, 1)

            def add_lora(b, pair):
                dve.wait_ge(s_lora, done(b, 2, pair + 1))
                if b.reg is not None or b.fixed >= 2:
                    dve.wait_ge(s_keep, done(b + -2, 1, 1))
                tt(h1[:, b.parity, 2 * pair:2 * pair + 2, :], emb[:, b.parity, 2 * pair:2 * pair + 2, 0:D],
                   misc_pair, ALU.add).then_inc(s_h1, 1)

            def norm_stats(which, x, ready, b, pair):
                dve.wait_ge(*ready)
                part = tiles(b, pair, which == 1)
                for c in range(part.start, part.stop):
                    last = nc.vector.bn_stats(ln[which][:, c, :], x[:, c, :])
                last.then_inc(s_stats[which], 1)
                dve.wait_ge(s_cst, 16)
                dve.wait_ge(s_stats[which], done(b, 2, pair + 1))
                for c in range(part.start, part.stop):
                    last = nc.vector.bn_aggr(ln_mv[which][:, c, :], ln[which][:, c, :])
                last.then_inc(s_mv[which], 1)

            def norm_apply(which, x, y, b, pair):
                dve.wait_ge(s_rstd[which], done(b, 2, pair + 1))
                part = tiles(b, pair, which == 1)
                for c in range(part.start, part.stop):
                    last = nc.vector.tensor_scalar(y[:, c, :], x[:, c, :], ln_mv[which][:, c, 0:1],
                                                   ln_rstd[which][:, c:c + 1], ALU.subtract, ALU.mult)
                last.then_inc(s_y[which], 1)

            def y_lo(which, hi, lo, b, pair):
                dve.wait_ge(s_yhi[which], done(b, 2, pair + 1))
                c = tiles(b, pair, which == 1)
                t = slice(c.start * P, c.stop * P)
                tt(lo[:, :, t], turned_part(which, b, c), hi[:, :, t].bitcast(F32),
                   ALU.subtract).then_inc(s_ylo[which], 1)

            def k_copies(b):
                dve.wait_ge(s_fk, done(b, 1, 1))
                nc.vector.tensor_copy(
                    k_rep[:, :, :].rearrange("p c (g n x) -> p (c g) n x", g=G, n=COPIES),
                    fk[:, :, :].rearrange("p c (g x) -> p (c g) x", g=G).unsqueeze(2)
                    .to_broadcast([P, C * G, COPIES, HG * FEAT])).then_inc(s_krep, 1)

            def q_over_den(b):
                dve.wait_ge(s_fq, done(b, 1, 1))
                dve.wait_ge(s_cumk, done(b, 1, 1))
                flat = lambda x: x[:, :, :].rearrange("p c n -> p (c n)")
                tt(flat(prod), flat(fq), sums_ps, ALU.mult).then_inc(s_prod, 1)
                dve.wait_ge(s_prod, done(b, 1, 1))
                pairs = flat(prod).rearrange("p (n f) -> p n f", f=FEAT)
                nc.vector.scalar_tensor_tensor(den[:, :], pairs[:, :, 0], DEN_EPS, pairs[:, :, 1], ALU.add,
                                               ALU.add).then_inc(s_den, 1)
                dve.wait_ge(s_den, done(b, 1, 1))
                nc.vector.reciprocal(rden[:, :], den[:, :]).then_inc(s_rden, 1)
                dve.wait_ge(s_rden, done(b, 1, 1))
                tt(flat(fqn).rearrange("p (n f) -> p n f", f=FEAT), flat(fq).rearrange("p (n f) -> p n f", f=FEAT),
                   rden[:, :].unsqueeze(2).to_broadcast([P, C * H, FEAT]), ALU.mult).then_inc(s_fqn, 1)
                dve.wait_ge(s_fqn, done(b, 1, 1))
                nc.vector.tensor_copy(
                    q_rep[:, :, :].rearrange("p c (g n x) -> p (c g) n x", g=G, n=COPIES),
                    fqn[:, :, :].rearrange("p c (g x) -> p (c g) x", g=G).unsqueeze(2)
                    .to_broadcast([P, C * G, COPIES, HG * FEAT])).then_inc(s_qrep, 1)

            def k_to_mix(b, first):
                dve.wait_ge(s_khi, done(b, 1, 1))
                if not first:
                    dve.wait_ge(s_kgrp, done(b + -1, 1, 1))
                stack(k_mix[:, :], round_hi[:, :], kt_ps, lo_k).then_inc(s_kmix, 1)

            def q_to_mix(b, first):
                dve.wait_ge(s_qhi, done(b, 1, 1))
                if not first:
                    dve.wait_ge(s_qgrp, done(b + -1, 1, 1))
                stack(q_mix[:, :], round_hi[:, :], qt_ps, lo_q).then_inc(s_qmix, 1)

            def q_heads(b):
                dve.wait_ge(s_qmix, done(b, 1, 1))
                for h in range(HG):
                    last = nc.vector.tensor_scalar(q_head[:, h, :], q_mix[:, :], cst[:, C_HEAD + h:C_HEAD + h + 1],
                                                   None, ALU.mult)
                last.then_inc(s_qhead, 1)

            def add_attention(b, pair):
                dve.wait_ge(s_omm, done(b, 2, pair + 1))
                dve.wait_ge(s_keep, done(b, 1, 1))
                c = tiles(b, pair)
                h = h2[:, c, :]
                tt(h, h, projected(b, c), ALU.add).then_inc(s_h2, 1)

            def mask(b, c, g):
                n = c * G + g
                dve.wait_ge(s_wmm, done(b, C * G, n + 1))
                if c >= 2:
                    dve.wait_ge(s_at, done(b, C * G, n - 2 * G + 1))
                tt(wts[:, c % 2, g * HG:(g + 1) * HG, :], ps[:, 5 + n % 2, :].rearrange("p (h t) -> p h t", t=P),
                   causal.unsqueeze(1).to_broadcast([P, HG, P]), ALU.mult).then_inc(s_wts, 1)

            def mask_state(b, c):
                dve.wait_ge(s_stmm, done(b, C - 1, c + 1))
                tt(st_mask[:, :, :], state_ps.rearrange("p (h e) -> p h e", e=E),
                   cst[:, C_HEAD:C_HEAD + HG].unsqueeze(2).to_broadcast([P, HG, E]), ALU.mult).then_inc(s_stm, 1)

            def state_to_stack(b, c):
                if c > 0:
                    dve.wait_ge(s_cross, done(b, C - 1, c))
                dve.wait_ge(s_sthi, done(b, C - 1, c + 1))
                stack(st[:, :], st_hi[:, :], st_mask[:, :, :].rearrange("p h e -> p (h e)"), lo_k).then_inc(s_st, 1)

            def heads_lo(b, c, half):
                dve.wait_ge(s_athi, done(b, 2 * C, 2 * c + half + 1))
                i = slice(4 * half, 4 * half + 4)
                tt(at_lo[:, i, c, :], heads_ps[:, i, :], at_hi[:, i, c, :].bitcast(F32), ALU.subtract)\
                    .then_inc(s_atlo, 1)

            def add_ffn(b, pair):
                dve.wait_ge(s_ffmm, done(b, 2, pair + 1))
                dve.wait_ge(s_h2b, done(b, 2, pair + 1))
                c = tiles(b, pair)
                o = outb[:, b.parity, c, :]
                tt(o, o, fed(b, pair)[:, 0:c.stop - c.start, :], ALU.add).then_inc(s_out, 1)

            nc.vector.sem_inc(s_out, 2)
            b0 = Batch(0)
            dve.wait_ge(s_lb, 16)
            nc.vector.tensor_scalar(lb2, raw_lb, LORA_SCALE, None, ALU.mult).then_inc(s_lb2, 1)
            dve.wait_ge(s_cst, 16)
            dve.wait_ge(s_lbhi, 1)
            stack(lb_all, round_hi[:, 0:D], lb2, lo_q).then_inc(s_lball, 1)
            dve.wait_ge(s_lball, 1)
            for c in range(C):
                last = nc.vector.tensor_scalar(lb_tiles[:, c, :], lb_all, cst[:, C_TILE + c:C_TILE + c + 1], None,
                                               ALU.mult)
            last.then_inc(s_lbs, 1)

            def weight_lo(n, lo, whole, hi, slabs):
                dve.wait_ge(s_whi, n)
                return tt(lo[:, slabs, :], whole[:, slabs, :], hi[:, slabs, :].bitcast(F32), ALU.subtract)

            a_copies(b0)
            a_to_stack(b0)
            weight_lo(1, wqkv_lo, raw_qkv, wqkv_hi, slice(0, 1))
            add_lora(b0, 0)
            norm_stats(0, h1[:, 0, :, :], (s_h1, 1), b0, 0)
            add_lora(b0, 1)
            norm_apply(0, h1[:, 0, :, :], y1, b0, 0)
            norm_stats(0, h1[:, 0, :, :], (s_h1, 2), b0, 1)
            weight_lo(2, wqkv_lo, raw_qkv, wqkv_hi, slice(1, KD)).then_inc(s_wdone, 1)
            y_lo(0, y1_hi, y1_lo, b0, 0)
            norm_apply(0, h1[:, 0, :, :], y1, b0, 1)
            dve.wait_ge(s_ff, 16)
            dve.wait_ge(s_low, 3)
            tt(raw_ff, raw_ff, low_pair, ALU.add).then_inc(s_wff, 1)
            y_lo(0, y1_hi, y1_lo, b0, 1)

            def run(b, first, last):
                prev, nxt = b + -1, b + 1
                x1 = h1[:, nxt.parity, :, :]

                def stats(which, pair):
                    if which == 0 and not last:
                        norm_stats(0, x1, (s_h1, done(nxt, 2, pair + 1)), nxt, pair)
                    if which == 1 and not first:
                        norm_stats(1, h2, (s_h2, done(prev, 2, pair + 1)), prev, pair)

                def apply(which, pair):
                    if which == 0 and not last:
                        norm_apply(0, x1, y1, nxt, pair)
                    if which == 1 and not first:
                        norm_apply(1, h2, y2, prev, pair)

                def lo(which, pair):
                    if which == 0 and not last:
                        y_lo(0, y1_hi, y1_lo, nxt, pair)
                    if which == 1 and not first:
                        y_lo(1, y2_hi, y2_lo, prev, pair)

                if not last:
                    a_copies(nxt)
                    a_to_stack(nxt)
                k_copies(b)
                q_over_den(b)
                k_to_mix(b, first)
                if not last:
                    add_lora(nxt, 0)
                q_to_mix(b, first)
                q_heads(b)
                stats(0, 0)
                mask(b, 0, 0)
                mask(b, 0, 1)
                if not last:
                    add_lora(nxt, 1)
                for c in range(C):
                    mask(b, c, 2)
                    mask(b, c, 3)
                    if c < 2:
                        apply(0, c)
                    if c == 2:
                        apply(1, 0)
                    if c < C - 1:
                        mask_state(b, c)
                    heads_lo(b, c, 0)
                    if c < C - 1:
                        state_to_stack(b, c)
                        if c == 0:
                            if not first:
                                add_attention(prev, 0)
                            lo(0, 0)
                        if c == 2 and first:
                            weight_lo(3, wo_lo, raw_wo, wo_hi, slice(0, PAIRS // 2))
                        mask(b, c + 1, 0)
                        mask(b, c + 1, 1)
                        if c == 0:
                            if not first:
                                add_attention(prev, 1)
                        if c == 1:
                            lo(0, 1)
                        if c == 2:
                            stats(1, 1)
                            lo(1, 0)
                    else:
                        lo(1, 1)
                        if first:
                            weight_lo(4, wff_lo, raw_ff, wff_hi, slice(0, KD)).then_inc(s_wdone, 1)
                    if c == 3 and last:
                        add_attention(b, 0)
                        norm_stats(1, h2, (s_h2, done(b, 2, 1)), b, 0)
                    if c == 3 and not first:
                        add_ffn(prev, 0)
                    heads_lo(b, c, 1)
                    if c == 0:
                        stats(0, 1)
                    if c == 1:
                        stats(1, 0)
                    if c == 2:
                        apply(1, 1)
                        if first:
                            weight_lo(3, wo_lo, raw_wo, wo_hi, slice(PAIRS // 2, PAIRS)).then_inc(s_wdone, 1)
                    if c == 3 and not first:
                        if last:
                            norm_apply(1, h2, y2, b, 0)
                            add_attention(b, 1)
                            norm_stats(1, h2, (s_h2, done(b, 2, 2)), b, 1)
                        add_ffn(prev, 1)
            iterations(dve, run)

            e = Batch(BATCHES - 1)
            y_lo(1, y2_hi, y2_lo, e, 0)
            norm_apply(1, h2, y2, e, 1)
            add_attention(e, 2)
            norm_stats(1, h2, (s_h2, done(e, 2, 3)), e, 2)
            y_lo(1, y2_hi, y2_lo, e, 1)
            add_ffn(e, 0)
            norm_apply(1, h2, y2, e, 2)
            y_lo(1, y2_hi, y2_lo, e, 2)
            add_ffn(e, 1)
            add_ffn(e, 2)


def constants():
    import numpy as np
    a = np.zeros((P, N_CONST), np.float32)
    row = np.arange(P)
    a[:, C_CAUSAL:C_CAUSAL + P] = row[:, None] <= row[None, :]
    a[:, C_ONES:C_ONES + P] = 1
    a[:, C_IDENT:C_IDENT + P] = np.eye(P)
    copy = row // (HG * FEAT) % COPIES
    a[:, C_LO_K] = -1.0 * (copy >= 2)
    a[:, C_LO_Q] = -1.0 * (copy % 2)
    for h in range(HG):
        a[:, C_HEAD + h] = row // FEAT % HG == h
    for c in range(C):
        a[:, C_TILE + c] = row // (COPIES * R) == c
    a[:, C_HALFPI] = np.pi / 2
    a[:, C_EPS] = LN_EPS
    a[:, C_POWER] = -0.5
    return a


def kernel(x, L0_tok_W, L0_tok_lora_A, L0_tok_lora_B, L0_attn_W_Q, L0_attn_W_K, L0_attn_W_V, L0_attn_W_O,
           L0_ffn_W, L0_ffn_b, L0_ffn_lora_down, L0_ffn_lora_up, L0_ffn_down_aux, L0_ffn_up_aux):
    import numpy as np
    import concourse.bacc as bacc
    from concourse.bass_utils import run_bass_kernel_spmd

    layout = {
        "idx": np.asarray(x).reshape(BATCHES * C, P).T,
        "table": np.concatenate([np.asarray(L0_tok_W), np.asarray(L0_tok_lora_A).T], axis=1),
        "wqkv": np.concatenate([np.asarray(L0_attn_W_V).transpose(1, 0, 2).reshape(D, HE),
                                np.asarray(L0_attn_W_Q)[:, :, 0].T, np.asarray(L0_attn_W_K)[:, :, 0].T], axis=1),
        "wo": np.asarray(L0_attn_W_O).transpose(2, 1, 0).reshape(HE, D),
        "wff": np.asarray(L0_ffn_W).T,
        "ld_t": np.asarray(L0_ffn_lora_down).T,
        "lu_t": np.asarray(L0_ffn_lora_up).T,
        "da": np.asarray(L0_ffn_down_aux),
        "ua_t": np.asarray(L0_ffn_up_aux).T,
        "lb_t": np.tile(np.asarray(L0_tok_lora_B).T, (C * COPIES, 1)),
        "bias": np.asarray(L0_ffn_b),
        "consts": constants(),
    }
    nc = bacc.Bacc("TRN2", target_bir_lowering=False, num_devices=1)
    arrays, args = {}, []
    for name, a in layout.items():
        a = np.ascontiguousarray(a)
        arrays[f"in_{name}"] = a
        args.append(nc.dram_tensor(f"in_{name}", a.shape, mybir.dt.from_np(a.dtype), kind="ExternalInput").ap())
    args.append(nc.dram_tensor("out_h", (BATCHES * T, D), F32, kind="ExternalOutput").ap())
    tower(nc, *args)
    r = run_bass_kernel_spmd(nc, [arrays], core_ids=[0])
    return r.results[0]["out_h"].reshape(BATCHES, T, D)
```
